# Optimizing a Trainium2 kernel written in Bass

```python
import numpy as np
import jax
import jax.numpy as jnp

def _softmax(x, axis=-1):
    return jax.nn.softmax(x, axis=axis)

def _gelu(x):
    return jax.nn.gelu(x, approximate=True)

def _silu(x):
    return jax.nn.silu(x)

def _sigmoid(x):
    return jax.nn.sigmoid(x)

def _layernorm(x, axis=-1, eps=1e-05):
    m = jnp.mean(x, axis=axis, keepdims=True)
    v = jnp.var(x, axis=axis, keepdims=True)
    return (x - m) / jnp.sqrt(v + eps)

def _scatter_add(tgt, idx, src, axis=0):
    return tgt.at[idx].add(src)

def _segment_sum(src, seg, n):
    return jax.ops.segment_sum(src, seg, n)
kernel_name = 'mk_adj_preln_d4_adj_r2_764bc6'

def setup_inputs(seed: int=0):
    np.random.seed(seed)
    _w = jnp.asarray

    def _rec_inputs():
        import jax
        import jax.numpy as jnp
        _gk = jax.random.key(seed)
        x = -0.0002928 + 1 * jax.random.normal(jax.random.fold_in(_gk, 1), (16, 512, 256), jnp.float32)
        _a = jax.random.bernoulli(jax.random.fold_in(_gk, 2), 0.0078125, (16, 512, 512))
        _a = jnp.logical_or(_a, jnp.swapaxes(_a, -1, -2))
        _a = jnp.logical_or(_a, jnp.eye(512, dtype=bool))
        _af = _a.astype(jnp.float32)
        _af = _af * jax.random.uniform(jax.random.fold_in(_gk, 3), (16, 512, 512), jnp.float32, 0.05, 1)
        adj = _af
        return (x, adj)
    x, adj = _rec_inputs()

    def _L0_gnn_setup():
        import jax, jax.numpy as jnp
        import numpy as np
        B, N, DIN, DOUT, K = (4, 1024, 256, 256, 3)
        key = jax.random.key(seed)
        ks = jax.random.split(key, 8)
        X = jax.random.normal(ks[0], (B, N, DIN), dtype=jnp.float32)
        A = jax.random.uniform(ks[1], (B, N, N), dtype=jnp.float32)
        Wv = jax.random.normal(ks[2], (DIN, DOUT), dtype=jnp.float32) * 0.02
        bv = jax.random.normal(ks[3], (DOUT,), dtype=jnp.float32) * 0.02
        aw = jax.random.normal(ks[4], (2 * DOUT, 1), dtype=jnp.float32) * 0.05
        ab = jax.random.normal(ks[5], (1,), dtype=jnp.float32) * 0.05
        Wk = jax.random.normal(ks[6], (K, DIN, DOUT), dtype=jnp.float32) * 0.02
        bk = jax.random.normal(ks[7], (K, DOUT), dtype=jnp.float32) * 0.02
        return {'X': X, 'A': A, 'Wv': Wv, 'bv': bv, 'aw': aw, 'ab': ab, 'Wk': Wk, 'bk': bk}
    _L0_gnn_all = _L0_gnn_setup()
    _L0_gnn_in = {k: v for k, v in _L0_gnn_all.items() if k in ('Wv', 'bv', 'aw', 'ab', 'Wk', 'bk')}
    del _L0_gnn_all

    def _L1_gnn_setup():
        import jax, jax.numpy as jnp
        import numpy as np
        B, N, D_IN, D_OUT = (4, 2048, 256, 256)
        key = jax.random.key(seed)
        k1, k2, k3, k4 = jax.random.split(key, 4)
        x = jax.random.normal(k1, (B, N, D_IN), dtype=jnp.float32)
        A_shape = jax.random.uniform(k2, (B, N, N), dtype=jnp.float32)
        w = jax.random.normal(k3, (D_IN, D_OUT), dtype=jnp.float32)
        a = jax.random.normal(k4, (D_OUT,), dtype=jnp.float32)
        return {'x': x, 'A_shape': A_shape, 'w': w, 'a': a}
    _L1_gnn_all = _L1_gnn_setup()
    _L1_gnn_in = {k: v for k, v in _L1_gnn_all.items() if k in ('w', 'a')}
    del _L1_gnn_all

    def _L2_gnn_setup():
        import jax, jax.numpy as jnp
        import numpy as np
        EMBED_DIM = 256
        NUM_HEADS = 8
        HEAD_DIM = EMBED_DIM // NUM_HEADS
        SCALE = HEAD_DIM ** (-0.5)
        B, S = (16, 512)
        key = jax.random.key(seed)
        ks = jax.random.split(key, 12)
        init = lambda k, shape: jax.random.normal(k, shape, dtype=jnp.float32) * EMBED_DIM ** (-0.5)
        return {'x': jax.random.normal(ks[0], (B, S, EMBED_DIM), dtype=jnp.float32), 'adj_matrix': jax.random.uniform(ks[1], (B, S, S), dtype=jnp.float32), 'bond_matrix': jax.random.uniform(ks[2], (B, S, S), dtype=jnp.float32), 'Wq': init(ks[3], (EMBED_DIM, EMBED_DIM)), 'bq': jnp.zeros((EMBED_DIM,), jnp.float32), 'Wk': init(ks[4], (EMBED_DIM, EMBED_DIM)), 'bk': jnp.zeros((EMBED_DIM,), jnp.float32), 'Wv': init(ks[5], (EMBED_DIM, EMBED_DIM)), 'bv': jnp.zeros((EMBED_DIM,), jnp.float32), 'Wo': init(ks[6], (EMBED_DIM, EMBED_DIM)), 'bo': jnp.zeros((EMBED_DIM,), jnp.float32), 'seq_len': S}
    _L2_gnn_all = _L2_gnn_setup()
    _L2_gnn_in = {k: v for k, v in _L2_gnn_all.items() if k in ('Wq', 'bq', 'Wk', 'bk', 'Wv', 'bv', 'Wo', 'bo')}
    del _L2_gnn_all

    def _L3_gnn_setup():
        import jax, jax.numpy as jnp
        import numpy as np
        EPS = 1e-06
        key = jax.random.key(seed)
        k1, k2, k3 = jax.random.split(key, 3)
        B, N, F, O = (8, 2048, 256, 256)
        x = jax.random.normal(k1, (B, N, F), dtype=jnp.float32)
        adj = jax.random.uniform(k2, (B, N, N), dtype=jnp.float32)
        W = jax.random.normal(k3, (O, 2 * F), dtype=jnp.float32) * (1.0 / np.sqrt(2 * F))
        return {'x': x, 'adj': adj, 'W': W}
    _L3_gnn_all = _L3_gnn_setup()
    _L3_gnn_in = {k: v for k, v in _L3_gnn_all.items() if k in ('W',)}
    del _L3_gnn_all
    return {'x': x, 'adj': adj, 'L0_gnn_Wv': _L0_gnn_in['Wv'], 'L0_gnn_bv': _L0_gnn_in['bv'], 'L0_gnn_aw': _L0_gnn_in['aw'], 'L0_gnn_ab': _L0_gnn_in['ab'], 'L0_gnn_Wk': _L0_gnn_in['Wk'], 'L0_gnn_bk': _L0_gnn_in['bk'], 'L1_gnn_w': _L1_gnn_in['w'], 'L1_gnn_a': _L1_gnn_in['a'], 'L2_gnn_Wq': _L2_gnn_in['Wq'], 'L2_gnn_bq': _L2_gnn_in['bq'], 'L2_gnn_Wk': _L2_gnn_in['Wk'], 'L2_gnn_bk': _L2_gnn_in['bk'], 'L2_gnn_Wv': _L2_gnn_in['Wv'], 'L2_gnn_bv': _L2_gnn_in['bv'], 'L2_gnn_Wo': _L2_gnn_in['Wo'], 'L2_gnn_bo': _L2_gnn_in['bo'], 'L3_gnn_W': _L3_gnn_in['W']}

def reference(x, adj, L0_gnn_Wv, L0_gnn_bv, L0_gnn_aw, L0_gnn_ab, L0_gnn_Wk, L0_gnn_bk, L1_gnn_w, L1_gnn_a, L2_gnn_Wq, L2_gnn_bq, L2_gnn_Wk, L2_gnn_bk, L2_gnn_Wv, L2_gnn_bv, L2_gnn_Wo, L2_gnn_bo, L3_gnn_W):
    import jax
    import jax.numpy as jnp

    def _L0_gnn_ref(X, A, Wv, bv, aw, ab, Wk, bk):
        import jax, jax.numpy as jnp
        import numpy as np
        B, N, DIN, DOUT, K = (4, 1024, 256, 256, 3)
        d = Wv.shape[1]
        Xw = X @ Wv + bv
        sj = Xw @ aw[:d, 0]
        si = Xw @ aw[d:, 0]
        e = jax.nn.leaky_relu(sj[:, None, :] + si[:, :, None] + ab[0], negative_slope=0.2)
        alpha_matrix = A * jnp.exp(e)
        transition = alpha_matrix / (jnp.sum(alpha_matrix, axis=-1, keepdims=True) + 1e-12)
        H = jnp.zeros(X.shape[:-1] + (d,), dtype=X.dtype)
        Xk = X
        for k in range(Wk.shape[0]):
            H = H + Xk @ Wk[k] + bk[k]
            Xk = jnp.einsum('bij,bjd->bid', transition, Xk)
        return jax.nn.relu(H)

    def _L1_gnn_ref(x, A_shape, w, a):
        import jax, jax.numpy as jnp
        import numpy as np
        B, N, D_IN, D_OUT = (4, 2048, 256, 256)
        y = x @ w
        s = y @ a
        A = s[..., :, None] + s[..., None, :]
        A = jnp.tanh(A / 8.0) * 8.0
        A = jnp.where(A >= 0, A, 0.1 * A)
        A = jnp.exp(A) * A_shape
        A = A / jnp.sum(A, axis=-1, keepdims=True)
        A = A * jnp.sum(A_shape, axis=-1, keepdims=True)
        out = A @ x @ w
        return out

    def _L2_gnn_ref(x, adj_matrix, bond_matrix, Wq, bq, Wk, bk, Wv, bv, Wo, bo, seq_len):
        import jax, jax.numpy as jnp
        import numpy as np
        EMBED_DIM = 256
        NUM_HEADS = 8
        HEAD_DIM = EMBED_DIM // NUM_HEADS
        SCALE = HEAD_DIM ** (-0.5)
        B, S = (16, 512)
        b = x.shape[0]

        def proj(W, bias):
            y = jnp.einsum('bse,fe->bsf', x, W) + bias
            return y.reshape(b, seq_len, NUM_HEADS, HEAD_DIM).transpose(0, 2, 1, 3)
        q, k, v = (proj(Wq, bq), proj(Wk, bk), proj(Wv, bv))
        scores = jnp.einsum('bhqd,bhkd->bhqk', q, k) * SCALE
        mask = (adj_matrix + bond_matrix)[:, None, :, :]
        scores = scores * mask
        attn = jax.nn.softmax(scores, axis=-1)
        ctx = jnp.einsum('bhqk,bhkd->bhqd', attn, v)
        ctx = ctx.transpose(0, 2, 1, 3).reshape(b, seq_len, EMBED_DIM)
        return jnp.einsum('bse,fe->bsf', ctx, Wo) + bo

    def _L3_gnn_ref(x, adj, W):
        import jax, jax.numpy as jnp
        import numpy as np
        EPS = 1e-06
        deg = jnp.sum(adj, axis=-1, keepdims=True)
        agg = jnp.einsum('bij,bjf->bif', adj, x) / jnp.maximum(deg, EPS)
        cat = jnp.concatenate([x, agg], axis=2)
        out = jnp.einsum('bnf,of->bno', cat, W)
        return jax.nn.relu(out)
    h = jnp.maximum(_layernorm(x, axis=-1), 0.0)
    x = x + _L0_gnn_ref(h, adj, L0_gnn_Wv, L0_gnn_bv, L0_gnn_aw, L0_gnn_ab, L0_gnn_Wk, L0_gnn_bk)
    h = jnp.maximum(_layernorm(x, axis=-1), 0.0)
    x = x + _L1_gnn_ref(h, adj, L1_gnn_w, L1_gnn_a)
    h = jnp.maximum(_layernorm(x, axis=-1), 0.0)
    x = x + _L2_gnn_ref(h, adj, adj, L2_gnn_Wq, L2_gnn_bq, L2_gnn_Wk, L2_gnn_bk, L2_gnn_Wv, L2_gnn_bv, L2_gnn_Wo, L2_gnn_bo, 512)
    h = jnp.maximum(_layernorm(x, axis=-1), 0.0)
    x = x + _L3_gnn_ref(h, adj, L3_gnn_W)
    return x

_drawn_inputs = setup_inputs


def setup_inputs(seed=0):
    import zlib

    import numpy as np

    out = dict(_drawn_inputs(seed))
    spreads = {'L2_gnn_bq': (0.0, 0.8),
     'L2_gnn_bk': (0.0, 2.0),
     'L2_gnn_bv': (0.0, 0.8),
     'L2_gnn_bo': (0.0, 2.0)}
    factors = {'L0_gnn_Wv': 8.0,
     'L0_gnn_bv': 8.0,
     'L0_gnn_aw': 8.0,
     'L2_gnn_Wq': 8.0,
     'L2_gnn_Wk': 8.0,
     'L2_gnn_Wv': 3.394,
     'L2_gnn_Wo': 3.444,
     'L3_gnn_W': 4.728}
    for name, (base, spread) in spreads.items():
        noise = np.random.default_rng([zlib.crc32(name.encode()), seed]).standard_normal(out[name].shape)
        drawn = base * np.exp(spread * noise) if base else spread * noise
        out[name] = jnp.asarray(drawn.astype(out[name].dtype))
    for name, factor in factors.items():
        out[name] = (out[name] * factor).astype(out[name].dtype)
    return out
```

```python
from contextlib import ExitStack

import concourse.bass as bass
from concourse import mybir

F32 = mybir.dt.float32
F32R = mybir.dt.float32r
ALU = mybir.AluOpType
ACT = mybir.ActivationFunctionType
AX_X = mybir.AxisListType.X

P = 128
B, N, D = 16, 512, 256
NT = N // P
DC = D // P
H = 8
HD = D // H
HG = P // HD
K0 = 3
LN_EPS = 1e-5
L0_EPS = 1e-12
L3_EPS = 1e-6
LOWEST = -3.0e38
MASK_SCALE = 2.0 * HD ** -0.5
SUB = H * NT

TURN_LAG = 5
PV_LAG = TURN_LAG + 3
CTX_LAG = PV_LAG + 1


def build_plan():
    order, core = [], [0]

    def attention(n):
        for _ in range(n):
            order.append(("core", core[0]))
            core[0] += 1

    def part(name, count=1, cores=0, every=1):
        for i in range(count):
            order.append((name, i))
            if cores and (i + 1) % every == 0:
                attention(1)
                cores -= 1

    part("stats0")
    attention(1)
    part("norm0")
    part("turn_h0")
    attention(2)
    part("g", NT, 4)
    part("si")
    part("e_low", NT)
    attention(1)
    part("e_max", NT)
    part("e_exp", NT)
    attention(2)
    part("out2", 2)
    part("stats3")
    attention(1)
    part("norm3")
    attention(1)
    part("turn_h3")
    attention(1)
    part("z", NT)
    part("adj3", NT, 2, 2)
    part("turn_adj", NT)
    part("alpha0", NT)
    attention(2)
    part("hop1", NT)
    attention(1)
    part("hop2", NT)
    part("stats1")
    attention(1)
    part("norm1")
    part("deg")
    attention(2)
    part("turn_h1")
    attention(1)
    part("y", NT)
    part("s1")
    attention(1)
    part("t_max", NT)
    attention(1)
    part("t_exp", NT)
    part("alpha1", NT)
    attention(1)
    part("agg1", NT)
    part("stats2")
    attention(2)
    part("norm2")
    attention(2)
    part("turn_h2")
    attention(1)
    part("qk", 2 * DC)
    part("v", NT // 2)
    attention(SUB - core[0])
    return order


PLAN = build_plan()
PREV = {"out2", "stats3", "norm3", "turn_h3", "z", "adj3"}
BANKS_OF = {"turn_h0": 2, "turn_h1": 2, "turn_h2": 2, "turn_h3": 2, "g": 2, "si": 1, "z": 1, "adj3": 1,
            "turn_adj": 1, "hop1": 1, "hop2": 1, "y": 1, "s1": 1, "agg1": 1, "qk": 1, "v": 1, "out2": 1}
BANK_USES = sum(BANKS_OF.get(name, 0) for name, _ in PLAN)
assert BANK_USES % 2 == 0 and sum(BANKS_OF.get(name, 0) for name, _ in PLAN if name in PREV) % 2 == 0

STACK_DMAS = HG * HG * 2
LAYERS = 4
RAW_LOADS = 15 + 2 * K0

PER_STEP = {
    "bank_0": BANK_USES // 2, "bank_1": BANK_USES // 2,
    "x_in": 16, "adj_in": 16, "stored": 16, "x_done": 1, "adj_masked": SUB, "scored": SUB,
    "stacks0": 16 * STACK_DMAS, "stacks1": 16 * STACK_DMAS,
    "scores": SUB, "bank_masked": SUB, "peaks": SUB, "shifted": SUB, "scores_turned": SUB,
    "turned": SUB, "bank_exp": SUB, "probs": SUB, "probs_used": SUB // HG, "summed": SUB // HG, "ctx_n": DC,
    "ctx_taken": DC, "var": LAYERS, "eps": LAYERS, "rstd": LAYERS, "h": LAYERS, "h2": LAYERS, "ht1": LAYERS * DC,
    "e_low": NT, "e_max": NT, "e_exp": NT, "alpha0": NT, "t_tanh": NT - 1, "t_max": NT, "t_exp": NT, "alpha1": NT,
    "q1": 2 * DC, "x_bias": 1, "x1": 1, "own": None,
}


class Tally:

    def __init__(self, own_per_step=0):
        self.count, self.turn = {}, None
        self.per_step = {**PER_STEP, "own": own_per_step}

    def add(self, name, more=1):
        self.count[name] = self.count.get(name, 0) + more

    def value(self, name, lag=0):
        n = self.count.get(name, 0) - lag
        if self.turn is None:
            return max(n, 0)
        assert n > 0, name
        return self.turn * (2 * self.per_step[name]) + n

    def enter_loop(self, turn):
        self.before, self.turn = dict(self.count), turn

    def leave_loop(self, turns):
        self.turn = None
        for name, n in self.count.items():
            added = n - self.before.get(name, 0)
            assert added == 2 * self.per_step[name], (name, added, self.per_step[name])
            self.count[name] = n + (turns - 1) * added


def gnn_program(nc, x_in, adj_in, Wv0, bv0, aw0, ab0, Wk0, bk0, w1, a1, Wq, bq, Wk, bk, Wv, bv, Wo, bo, W3, out):
    with ExitStack() as ctx:
        def sb(name, shape, dt=F32):
            return ctx.enter_context(nc.sbuf_tensor(name, shape, dt))

        def bank(name):
            return ctx.enter_context(nc.psum_tensor(name, [P, N], F32))

        def sem(name):
            return ctx.enter_context(nc.semaphore(name))

        adj = [sb(f"adj{i}", [P, NT, N]) for i in range(2)]
        adj_t = [sb(f"adj_t{i}", [P, NT, N]) for i in range(2)]
        x = [sb(f"x{i}", [P, NT, D]) for i in range(2)]
        x_raw = sb("x_raw", [P, NT, D])
        v = [sb(f"v{i}", [P, NT, D]) for i in range(2)]
        deg = sb("deg", [P, 2, NT])
        alpha = sb("alpha", [P, NT, N])
        gg = sb("gg", [P, NT, 2 * D + 1])
        g0 = sb("g0", [P, NT, D])
        u = sb("u", [P, NT, D])
        h = u[:, :, :]
        ht1 = sb("ht1", [P, DC, N], F32R)
        ht2 = sb("ht2", [P, DC, N], F32R)
        z = sb("z", [P, NT, 2 * D])
        si = z[:, NT - 1, :]
        q_part = [alpha[:, 0:2, :], alpha[:, 2:4, :]]
        k_part = [g0[:, :, :].rearrange("p a b -> p (a b)").rearrange("p (a b) -> p a b", a=DC),
                  gg[:, :, 0:D].rearrange("p (c t) n -> p c t n", c=DC)]
        q_stack = [sb(f"q_stack{c}", [P, HG, N], F32R) for c in range(DC)]
        k_stack = [sb(f"k_stack{c}", [P, HG, N], F32R) for c in range(DC)]
        scores = sb("scores", [P, 2, NT, N])
        probs = sb("probs", [P, HG, NT, N])
        ctx_n = sb("ctx_n", [P, DC, N])
        stats = sb("stats", [P, NT, 6])
        mean_var = sb("mean_var", [P, NT, 2])
        rstd = sb("rstd", [P, NT])
        var_eps = sb("var_eps", [P, NT])
        minus_half = sb("minus_half", [P, NT])
        peak = sb("peak", [P, 2 * NT])
        sj = sb("sj", [P, NT])
        sj_low = sb("sj_low", [P, NT])
        s8 = sb("s8", [P, NT])
        rs = sb("rs", [P, NT])
        rinv = sb("rinv", [P, NT])
        dinv = sb("dinv", [P, NT])
        dmax = sb("dmax", [P, NT])
        WG = 3 * D + 2
        wg = [sb(f"wg{i}", [P, DC, WG], F32R) for i in range(2)]
        wy = [sb(f"wy{i}", [P, DC, D + 2], F32R) for i in range(2)]
        w_si = [sb(f"w_si{i}", [P, DC, P], F32R) for i in range(2)]
        w_s1 = [sb(f"w_s1{i}", [P, DC, P], F32R) for i in range(2)]
        wqkv = [sb(f"wqkv{i}", [P, DC, 3 * D], F32R) for i in range(2)]
        w3t = [sb(f"w3t{i}", [P, DC, 2 * D], F32R) for i in range(2)]
        wo_t = sb("wo_t", [P, DC, D])
        bias0 = sb("bias0", [P, D])
        bias_v = sb("bias_v", [P, D])
        bias_o = sb("bias_o", [P, D])
        bias_qk = sb("bias_qk", [P, 2, DC])
        e_const = sb("e_const", [P, 1])
        col = sb("col", [P, 3, DC])
        dots = sb("dots", [P, 3])
        ident = sb("ident", [P, P])
        ones = sb("ones", [P, HD])
        raw = probs[:, :, :, :].rearrange("p a b c -> p (a b c)")
        at = [0]

        def room(n):
            at[0] += n
            return raw[:, at[0] - n:at[0]]

        raw_k0 = room(K0 * DC * D).rearrange("p (k c n) -> p k c n", k=K0, c=DC)
        raw_v0 = room(DC * D).rearrange("p (c n) -> p c n", c=DC)
        raw_w1 = room(DC * D).rearrange("p (c n) -> p c n", c=DC)
        raw_qkvo = room(4 * DC * D).rearrange("p (m c n) -> p m c n", m=4, c=DC)
        raw_w3 = room(DC * 2 * D).rearrange("p (c n) -> p c n", c=DC)
        raw_aw = room(2 * D)
        raw_bv0 = room(D)
        raw_a1 = room(D)
        raw_bk0 = room(K0 * D).rearrange("p (k n) -> p k n", k=K0)
        raw_ab = room(1)
        junk = z[:, 0, 0:D]
        one_block = z[:, 1, 0:P]

        score_bank = [bank("score_bank0"), bank("score_bank1")]
        turn_bank = [bank("turn_bank0"), bank("turn_bank1")]
        ctx_bank = bank("ctx_bank")
        sum_bank = bank("sum_bank")
        shared = [bank("shared0"), bank("shared1")]

        s_x_in = sem("s_x_in")
        s_adj_in = sem("s_adj_in")
        s_stacks = [sem(f"s_stacks{c}") for c in range(DC)]
        s_stored = sem("s_stored")
        s_scores = sem("s_scores")
        s_peaks = sem("s_peaks")
        s_shifted = sem("s_shifted")
        s_turned = sem("s_turned")
        s_probs = sem("s_probs")
        s_probs_used = sem("s_probs_used")
        s_ctx_n = sem("s_ctx_n")
        s_q1 = sem("s_q1")
        s_x_bias = sem("s_x_bias")
        s_var = sem("s_var")
        s_eps = sem("s_eps")
        s_rstd = sem("s_rstd")
        s_h = sem("s_h")
        s_ht1 = sem("s_ht1")
        s_e_low = sem("s_e_low")
        s_e_max = sem("s_e_max")
        s_e_exp = sem("s_e_exp")
        s_alpha0 = sem("s_alpha0")
        s_t_tanh = sem("s_t_tanh")
        s_t_max = sem("s_t_max")
        s_t_exp = sem("s_t_exp")
        s_alpha1 = sem("s_alpha1")
        s_x1 = sem("s_x1")
        s_x_done = sem("s_x_done")
        s_own = sem("s_own")
        s_bank_full = [sem(f"s_bank_full{b}") for b in range(2)]
        s_bank_read = [sem(f"s_bank_read{b}") for b in range(2)]
        s_raw = sem("s_raw")
        s_passed = sem("s_passed")
        s_clear = sem("s_clear")
        s_ident = sem("s_ident")
        s_half = sem("s_half")
        s_wt = sem("s_wt")
        s_wt_read = sem("s_wt_read")
        s_weights = sem("s_weights")

        class Walk:

            def __init__(self, eng, own_per_step=0):
                self.eng, self.n, self.uses = eng, Tally(own_per_step), 0

            def due(self, name, more=0, lag=0):
                self.n.add(name, more)
                return self.n.value(name, lag)

            def pass_over(self, name, more=1):
                self.n.add(name, more)

            def own(self):
                self.n.add("own")
                return 1

            def stand_apart(self):
                if self.n.turn is not None:
                    self.eng.sem_inc(s_passed, 1)

            def take_bank(self):
                b = self.uses % 2
                self.uses += 1
                self.n.add(f"bank_{b}")
                return b

            def uses_of(self, b, lag=0):
                return self.n.value(f"bank_{b}", lag)

            def pass_by(self, name):
                for _ in range(BANKS_OF.get(name, 0)):
                    self.take_bank()

            def run(self, step):
                step(-1, 1, False, False, True)
                step(0, 0, False, True, True)
                turns = (B - 4) // 2
                with self.eng.Fori(0, turns) as turn:
                    self.n.enter_loop(turn)
                    step(1 + 2 * turn, 1, True, True, True)
                    step(2 + 2 * turn, 0, True, True, True)
                self.n.leave_loop(turns)
                step(B - 3, 1, True, True, True)
                step(B - 2, 0, True, True, True)
                step(B - 1, 1, True, True, False)
                step(B, 0, True, False, False)

        def parts(prev, nxt):
            for name, i in PLAN:
                if name == "core" or (prev if name in PREV else nxt):
                    yield name, i

        def lagged(j, lag, prev, now):
            head, r = divmod((j - lag) % SUB, NT)
            return head, r, j < lag, (prev if j < lag else now)

        block = ctx.enter_context(nc.Block())

        @block.sync
        def _(sp):
            def rows(vector, count):
                return vector.rearrange("(o n) -> o n", o=1).to_broadcast([P, count])

            with nc.allow_non_contiguous_dma(reason="small vectors, once"):
                for dst, src in (
                    (raw_qkvo[:, 0, :, :], Wq.rearrange("(c p) n -> p c n", p=P)),
                    (raw_qkvo[:, 1, :, :], Wk.rearrange("(c p) n -> p c n", p=P)),
                    (raw_qkvo[:, 2, :, :], Wv.rearrange("(c p) n -> p c n", p=P)),
                    (raw_qkvo[:, 3, :, :], Wo.rearrange("(c p) n -> p c n", p=P)),
                    (raw_w3, W3.rearrange("(c p) n -> p c n", p=P)),
                    (raw_v0, Wv0.rearrange("(c p) n -> p c n", p=P)),
                    (raw_w1, w1.rearrange("(c p) n -> p c n", p=P)),
                    (raw_aw, aw0.rearrange("n o -> o n").to_broadcast([P, 2 * D])),
                    (raw_bv0, rows(bv0, D)),
                    (raw_a1, rows(a1, D)),
                    (raw_ab, rows(ab0, 1)),
                    (bias_v[:, :], rows(bv, D)),
                    (bias_o[:, :], rows(bo, D)),
                    (bias_qk[:, 0, :], bq.rearrange("(c p) -> p c", p=P)),
                    (bias_qk[:, 1, :], bk.rearrange("(c p) -> p c", p=P)),
                ):
                    sp.dma_start(dst, src).then_inc(s_raw, 16)
                for k in range(K0):
                    sp.dma_start(raw_k0[:, k, :, :], Wk0[k].rearrange("(c p) n -> p c n", p=P)).then_inc(s_raw, 16)
                    sp.dma_start(raw_bk0[:, k, :], bk0[k:k + 1, :].to_broadcast([P, D])).then_inc(s_raw, 16)

            x_v = x_in.rearrange("b (t p) d -> b p t d", p=P)
            adj_v = adj_in.rearrange("b (t p) n -> b p t n", p=P)
            out_v = out.rearrange("b (t p) d -> b p t d", p=P)

            def of_graph(view, g):
                if isinstance(g, int):
                    return view[g]
                return view[bass.ds(g, 1)].rearrange("o p t n -> (o p) t n")

            w = Walk(sp)

            def step(t, par, prev, now, nxt):
                if nxt:
                    sp.wait_ge(s_peaks, w.due("adj_masked", SUB, 2 * SUB))
                    w.stand_apart()
                    sp.dma_start(adj[1 - par][:, :, :], of_graph(adj_v, t + 1)).then_inc(s_adj_in, 16)
                if isinstance(t, int) and t == -1:
                    sp.dma_start(x_raw[:, :, :], of_graph(x_v, 0)).then_inc(s_x_in, 16)
                for name, i in parts(prev, nxt):
                    if name == "stats1" and not (isinstance(t, int) and t + 2 >= B):
                        sp.wait_ge(s_x1, w.due("x1", 1))
                        w.stand_apart()
                        sp.dma_start(x_raw[:, :, :], of_graph(x_v, t + 2)).then_inc(s_x_in, 16)
                    if name == "qk":
                        w.take_bank()
                        if i % 2 == 0:
                            continue
                        c = i // 2
                        for b in range(2):
                            sp.wait_ge(s_bank_read[b], w.uses_of(b))
                            w.stand_apart()
                        sp.wait_ge(s_scores, w.due("scored", SUB // DC, SUB))
                        w.stand_apart()
                        for j in range(HG):
                            rows_j = slice(j * HD, (j + 1) * HD)
                            for g in range(HG):
                                rows_g = slice(g * HD, (g + 1) * HD)
                                sp.dma_start(q_stack[c][rows_j, g, :].bitcast(F32), q_part[j // 2][rows_g, c, :])\
                                    .then_inc(s_stacks[c], 16)
                                k_to, k_from = k_stack[c][rows_j, g, :].bitcast(F32), k_part[j % 2][rows_g, c]
                                if j % 2:
                                    k_to = k_to.rearrange("p (t n) -> p t n", n=D)
                                sp.dma_start(k_to, k_from).then_inc(s_stacks[c], 16)
                        continue
                    w.pass_by(name)
                    if name == "adj3" and i == NT - 1:
                        sp.wait_ge(s_x_done, w.due("x_done", 1))
                        w.stand_apart()
                        sp.dma_start(of_graph(out_v, t - 1), x[1 - par][:, :, :]).then_inc(s_stored, 16)

            w.run(step)
            sp.wait_ge(s_stored, 16 * B)

        @block.tensor
        def _(pe):
            pe.wait_ge(s_ident, 1)
            pe.wait_ge(s_raw, 16 * RAW_LOADS)
            turns = [(raw_qkvo[:, m, :, :], ec) for m in range(4) for ec in range(DC)]
            turns += [(raw_w3, ec) for ec in range(2 * DC)]
            for n, (weight, ec) in enumerate(turns):
                if n >= 2:
                    pe.wait_ge(s_wt_read, n - 1)
                for c in range(DC):
                    last = pe.transpose(shared[n % 2][:, c * P:(c + 1) * P], weight[:, c, ec * P:(ec + 1) * P],
                                        ident[:, :])
                last.then_inc(s_wt, 1)
            pe.wait_ge(s_weights, 1)

            w = Walk(pe)
            ht = (ht1, ht2)

            def product3(to, left, right):
                terms = [(c, a, b) for c in range(DC) for a, b in ((0, 0), (0, 1), (1, 0))]
                for n, (c, a, b) in enumerate(terms):
                    last = pe.matmul(to, left(a, c), right(b, c), start=(n == 0), stop=(n == len(terms) - 1))
                return last

            def nodes(i):
                return lambda a, c: ht[a][:, c, i * P:(i + 1) * P]

            def all_nodes(a, c):
                return ht[a][:, c, :]

            def columns(weight, lo, hi):
                return lambda a, c: weight[a][:, c, lo:hi]

            def product_bank(cols, left, right):
                b = w.take_bank()
                pe.wait_ge(s_bank_read[b], w.uses_of(b, 1))
                product3(shared[b][:, 0:cols], left, right).then_inc(s_bank_full[b], 1)

            def aggregate(i, weights, values):
                b = w.take_bank()
                pe.wait_ge(s_bank_read[b], w.uses_of(b, 1))
                to = shared[b][:, 0:values.shape[-1]]
                for j in range(NT):
                    last = pe.matmul(to, weights[:, j, i * P:(i + 1) * P], values[:, j, :],
                                     start=(j == 0), stop=(j == NT - 1))
                last.then_inc(s_bank_full[b], 1)

            def core(j, par, prev, now):
                head, r, _, exists = lagged(j, 0, prev, now)
                if exists:
                    c = head // HG
                    if head % HG == 0 and r == 0:
                        pe.wait_ge(s_stacks[c], w.due(f"stacks{c}", 16 * STACK_DMAS))
                    pe.wait_ge(s_peaks, w.due("bank_masked", 1, 2))
                    pe.matmul(score_bank[j % 2][:, :], q_stack[c][:, head % HG, r * P:(r + 1) * P],
                              k_stack[c][:, head % HG, :], start=True, stop=True).then_inc(s_scores, 1)
                head, c, _, exists = lagged(j, TURN_LAG, prev, now)
                if exists:
                    if c == 0:
                        pe.wait_ge(s_shifted, w.due("shifted", NT))
                    pe.wait_ge(s_probs, w.due("bank_exp", 1, 2))
                    for r in range(NT):
                        last = pe.transpose(turn_bank[(j - TURN_LAG) % 2][:, r * P:(r + 1) * P],
                                            scores[:, head % 2, r, c * P:(c + 1) * P], ident[:, :])
                    last.then_inc(s_turned, 1)
                head, c, older, exists = lagged(j, PV_LAG, prev, now)
                if exists and head % HG == HG - 1:
                    group = head // HG
                    values = v[1 - par] if older else v[par]
                    if c == 0:
                        pe.wait_ge(s_ctx_n, w.due("ctx_taken", 1, 1))
                    pe.wait_ge(s_probs, w.due("probs", (HG - 1) * NT + 1 if c == 0 else 1))
                    for g in range(HG):
                        rows_g = slice(g * HD, (g + 1) * HD)
                        pe.matmul(ctx_bank[rows_g, :], values[:, c, group * P + g * HD:group * P + (g + 1) * HD],
                                  probs[:, g, c, :], start=(c == 0), stop=(c == NT - 1))
                    for g in range(HG):
                        rows_g = slice(g * HD, (g + 1) * HD)
                        last = pe.matmul(sum_bank[rows_g, :], ones[:, :], probs[:, g, c, :],
                                         start=(c == 0), stop=(c == NT - 1))
                    last.then_inc(s_probs_used, 1)

            def step(t, par, prev, now, nxt):
                for name, i in parts(prev, nxt):
                    if name == "core":
                        core(i, par, prev, now)
                    elif name.startswith("turn_h"):
                        pe.wait_ge(s_h, w.due("h", 1))
                        for c in range(DC):
                            b = w.take_bank()
                            pe.wait_ge(s_bank_read[b], w.uses_of(b, 1))
                            for r in range(NT):
                                last = pe.transpose(shared[b][:, r * P:(r + 1) * P], h[:, r, c * P:(c + 1) * P],
                                                    ident[:, :])
                            last.then_inc(s_bank_full[b], 1)
                    elif name == "g":
                        if i == 0:
                            for b in range(2):
                                pe.wait_ge(s_bank_read[b], w.uses_of(b))
                        product_bank(2 * D, nodes(i), columns(wg, 0, 2 * D))
                        product_bank(D + 2, nodes(i), columns(wg, 2 * D, WG))
                    elif name == "si":
                        product_bank(N, columns(w_si, 0, P), all_nodes)
                    elif name == "turn_adj":
                        if i == 0:
                            pe.wait_ge(s_adj_in, w.due("adj_in", 16))
                        b = w.take_bank()
                        pe.wait_ge(s_bank_read[b], w.uses_of(b, 1))
                        for r in range(NT):
                            last = pe.transpose(shared[b][:, r * P:(r + 1) * P], adj[1 - par][:, r, i * P:(i + 1) * P],
                                                ident[:, :])
                        last.then_inc(s_bank_full[b], 1)
                    elif name == "hop1":
                        if i == 0:
                            pe.wait_ge(s_alpha0, w.due("alpha0", NT))
                        aggregate(i, alpha, gg[:, :, D:2 * D + 1])
                    elif name == "hop2":
                        if i == 0:
                            for b in range(2):
                                pe.wait_ge(s_bank_read[b], w.uses_of(b))
                        aggregate(i, alpha, u[:, :, :])
                    elif name == "y":
                        if i == 0:
                            for b in range(2):
                                pe.wait_ge(s_bank_read[b], w.uses_of(b))
                        product_bank(D + 2, nodes(i), columns(wy, 0, D + 2))
                    elif name == "s1":
                        product_bank(N, columns(w_s1, 0, P), all_nodes)
                    elif name == "agg1":
                        if i == 0:
                            pe.wait_ge(s_alpha1, w.due("alpha1", NT))
                        aggregate(i, alpha, gg[:, :, D:2 * D + 1])
                    elif name == "qk":
                        if i == 0:
                            for b in range(2):
                                pe.wait_ge(s_bank_read[b], w.uses_of(b))
                        c, m = divmod(i, 2)
                        product_bank(N, columns(wqkv, m * D + c * P, m * D + (c + 1) * P), all_nodes)
                    elif name == "v":
                        b = w.take_bank()
                        pe.wait_ge(s_bank_read[b], w.uses_of(b, 1))
                        for k in range(2):
                            last = product3(shared[b][:, k * D:(k + 1) * D], nodes(2 * i + k),
                                            columns(wqkv, 2 * D, 3 * D))
                        last.then_inc(s_bank_full[b], 1)
                    elif name == "out2":
                        if i == 0:
                            pe.wait_ge(s_ctx_n, w.due("ctx_n", DC))
                        b = w.take_bank()
                        pe.wait_ge(s_bank_read[b], w.uses_of(b, 1))
                        for k in range(2):
                            q = (2 * i + k) * P
                            for c in range(DC):
                                last = pe.matmul(shared[b][:, k * D:(k + 1) * D], ctx_n[:, c, q:q + P], wo_t[:, c, :],
                                                 start=(c == 0), stop=(c == DC - 1))
                        last.then_inc(s_bank_full[b], 1)
                    elif name == "z":
                        if i == 0:
                            for b in range(2):
                                pe.wait_ge(s_bank_read[b], w.uses_of(b))
                        product_bank(2 * D, nodes(i), columns(w3t, 0, 2 * D))
                    elif name == "adj3":
                        if i == 0:
                            for b in range(2):
                                pe.wait_ge(s_bank_read[b], w.uses_of(b))
                        aggregate(i, adj_t[1 - par], z[:, :, D:2 * D])

            w.run(step)

        @block.scalar
        def _(act):
            act.wait_ge(s_raw, 16 * RAW_LOADS)
            w = Walk(act)

            def step(t, par, prev, now, nxt):
                for name, i in parts(prev, nxt):
                    if name == "core":
                        head, c, _, exists = lagged(i, TURN_LAG, prev, now)
                        if exists:
                            act.wait_ge(s_turned, w.due("turned", 1))
                            if head % HG == 0:
                                act.wait_ge(s_probs_used, w.due("probs_used", 1, NT))
                            act.activation(probs[:, head % HG, c, :], turn_bank[(i - TURN_LAG) % 2][:, :], ACT.Exp,
                                           scale=-1.0).then_inc(s_probs, 1)
                    elif name.startswith("turn_h"):
                        for c in range(DC):
                            b = w.take_bank()
                            act.wait_ge(s_bank_full[b], w.uses_of(b))
                            act.activation(ht1[:, c, :], shared[b][:, :], ACT.Relu).then_inc(s_ht1, 1)
                    elif name == "g":
                        if i == 0 and (prev or now):
                            for c in range(DC):
                                act.wait_ge(s_stacks[c], w.due(f"stacks{c}", 16 * STACK_DMAS))
                        b = w.take_bank()
                        act.wait_ge(s_bank_full[b], w.uses_of(b))
                        act.copy(gg[:, i, 0:2 * D], shared[b][:, :]).then_inc(s_bank_read[b], 1)
                        w.take_bank()
                    elif name == "si":
                        for b in range(2):
                            act.wait_ge(s_bank_read[b], w.uses_of(b))
                        b = w.take_bank()
                        act.wait_ge(s_bank_full[b], w.uses_of(b))
                        act.copy(si[:, :], shared[b][:, :]).then_inc(s_bank_read[b], 1)
                        for b in range(2):
                            act.wait_ge(s_bank_read[b], w.uses_of(b))
                    elif name == "e_low":
                        act.activation(alpha[:, i, :], si[:, :], ACT.Identity, scale=0.2,
                                       bias=sj_low[:, i:i + 1]).then_inc(s_e_low, 1)
                    elif name == "e_exp":
                        act.wait_ge(s_e_max, w.due("e_max", 1))
                        act.activation(alpha[:, i, :], alpha[:, i, :], ACT.Exp).then_inc(s_e_exp, 1)
                    elif name == "turn_adj":
                        b = w.take_bank()
                        act.wait_ge(s_bank_full[b], w.uses_of(b))
                        act.copy(adj_t[1 - par][:, i, :], shared[b][:, :]).then_inc(s_bank_read[b], 1)
                    elif name == "y":
                        b = w.take_bank()
                        act.wait_ge(s_bank_full[b], w.uses_of(b))
                        act.copy(gg[:, i, D:2 * D], shared[b][:, 0:D])
                        act.mul(s8[:, i:i + 1], shared[b][:, D:D + 1], 0.125).then_inc(s_bank_read[b], 1)
                    elif name == "s1":
                        for b in range(2):
                            act.wait_ge(s_bank_read[b], w.uses_of(b))
                        b = w.take_bank()
                        act.wait_ge(s_bank_full[b], w.uses_of(b))
                        for j in range(NT):
                            tanh = act.activation(alpha[:, j, :], shared[b][:, :], ACT.Tanh, scale=0.125,
                                                  bias=s8[:, j:j + 1])
                            if j < NT - 1:
                                tanh.then_inc(s_t_tanh, 1)
                            else:
                                tanh.then_inc(s_bank_read[b], 1)
                    elif name == "t_exp":
                        act.wait_ge(s_t_max, w.due("t_max", 1))
                        act.activation(alpha[:, i, :], alpha[:, i, :], ACT.Exp, scale=8.0).then_inc(s_t_exp, 1)
                    elif name == "qk":
                        c, m = divmod(i, 2)
                        b = w.take_bank()
                        act.wait_ge(s_bank_full[b], w.uses_of(b))
                        part = (q_part, k_part)[m][0]
                        act.activation(part[:, c, :].bitcast(F32R), shared[b][:, :], ACT.Identity,
                                       bias=bias_qk[:, m, c:c + 1]).then_inc(s_q1, 1)
                    elif name == "z":
                        b = w.take_bank()
                        act.wait_ge(s_bank_full[b], w.uses_of(b))
                        act.copy(z[:, i, :], shared[b][:, :]).then_inc(s_bank_read[b], 1)
                    else:
                        w.pass_by(name)

            w.run(step)

        @block.gpsimd
        def _(pool):
            pool.memset(ident[:, :], 0.0).then_inc(s_clear, 1)
            pool.wait_ge(s_clear, 1)
            pool.affine_select(out=ident[:, :], in_=ident[:, :], compare_op=ALU.not_equal, fill=1.0, base=0,
                               pattern=[[-1, P]], channel_multiplier=1).then_inc(s_ident, 1)
            pool.memset(minus_half[:, :], -0.5).then_inc(s_half, 1)
            pool.wait_ge(s_half, 1)
            pool.wait_ge(s_raw, 16 * RAW_LOADS)
            w = Walk(pool)

            def step(t, par, prev, now, nxt):
                for name, i in parts(prev, nxt):
                    if name == "core" and now:
                        head, r = divmod(i, NT)
                        tile = scores[:, head % 2, r, :]
                        pool.wait_ge(s_peaks, w.due("peaks", 1))
                        w.stand_apart()
                        pool.tensor_scalar(tile, tile, -1.0, peak[:, i % (2 * NT):i % (2 * NT) + 1],
                                           ALU.mult, ALU.add).then_inc(s_shifted, 1)
                    elif name.startswith("stats"):
                        pool.wait_ge(s_var, w.due("var", 1))
                        w.stand_apart()
                        pool.tensor_scalar(var_eps[:, :], mean_var[:, :, 1], LN_EPS, 0.0, ALU.add, ALU.add)\
                            .then_inc(s_eps, 1)
                        pool.wait_ge(s_eps, w.due("eps", 1))
                        pool.tensor_tensor(rstd[:, :], var_eps[:, :], minus_half[:, :], ALU.pow).then_inc(s_rstd, 1)
                    elif name.startswith("norm"):
                        w.pass_over("h2")
                        if name != "norm2":
                            continue
                        pool.wait_ge(s_h, w.due("h2"))
                        xt = x[1 - par][:, :, :]
                        pool.tensor_tensor(xt, xt, bias_o[:, :].rearrange("p (o n) -> p o n", o=1)
                                           .to_broadcast([P, NT, D]), ALU.add).then_inc(s_x_bias, 1)

            w.run(step)

        @block.vector
        def _(dve):
            own_per_step = LAYERS * NT + 2 * NT + 2 * NT + 2 * NT + 3 + DC
            w = Walk(dve, own_per_step)

            dve.wait_ge(s_raw, 16 * RAW_LOADS)
            dve.memset(ones[:, :], 1.0).then_inc(s_own, w.own())
            dve.memset(one_block, 1.0).then_inc(s_own, w.own())
            dve.memset(gg[:, :, 2 * D:2 * D + 1], 1.0).then_inc(s_own, w.own())
            for part in range(2):
                dve.memset(wg[part][:, :, WG - 1:WG].bitcast(F32), 0.0).then_inc(s_own, w.own())
                dve.memset(wy[part][:, :, D + 1:D + 2].bitcast(F32), 0.0).then_inc(s_own, w.own())
            for c in range(DC):
                for n, (a, b) in enumerate(((raw_v0, raw_aw[:, 0:D]), (raw_v0, raw_aw[:, D:2 * D]), (raw_w1, raw_a1))):
                    dve.tensor_tensor_reduce(junk, a[:, c, :], b, 1.0, 0.0, ALU.mult, ALU.add,
                                                 col[:, n, c:c + 1]).then_inc(s_own, w.own())
                    dve.wait_ge(s_own, w.due("own"))
            for n in range(2):
                dve.tensor_tensor_reduce(junk, raw_bv0, raw_aw[:, n * D:(n + 1) * D], 1.0, 0.0, ALU.mult, ALU.add,
                                             dots[:, n:n + 1]).then_inc(s_own, w.own())
                dve.wait_ge(s_own, w.due("own"))
            dve.tensor_tensor(dots[:, 2:3], dots[:, 0:1], dots[:, 1:2], ALU.add).then_inc(s_own, w.own())
            dve.tensor_tensor(bias0[:, :], raw_bk0[:, 0, :], raw_bk0[:, 1, :], ALU.add).then_inc(s_own, w.own())
            dve.wait_ge(s_own, w.due("own"))
            dve.tensor_tensor(e_const[:, :], dots[:, 2:3], raw_ab, ALU.add).then_inc(s_own, w.own())
            dve.tensor_tensor(bias0[:, :], bias0[:, :], raw_bk0[:, 2, :], ALU.add).then_inc(s_own, w.own())
            split = []
            for c in range(DC):
                for k, at_col in ((1, 0), (2, D), (0, 2 * D)):
                    split.append((wg, (c, at_col, D), raw_k0[:, k, c, :]))
                split.append((wg, (c, 3 * D, 1), col[:, 0, c:c + 1]))
                split.append((wy, (c, 0, D), raw_w1[:, c, :]))
                split.append((wy, (c, D, 1), col[:, 2, c:c + 1]))
            for weight, (c, lo, n), src in split:
                dve.tensor_copy(weight[0][:, c, lo:lo + n], src).then_inc(s_own, w.own())
            for c in range(DC):
                dve.tensor_scalar(w_si[0][:, c, :], one_block, col[:, 1, c:c + 1], None, ALU.mult).then_inc(s_own, w.own())
                dve.tensor_scalar(w_s1[0][:, c, :], one_block, col[:, 2, c:c + 1], None, ALU.mult).then_inc(s_own, w.own())
            dve.wait_ge(s_own, w.due("own"))
            for weight, (c, lo, n), src in split:
                dve.tensor_tensor(weight[1][:, c, lo:lo + n], src, weight[0][:, c, lo:lo + n].bitcast(F32),
                                      ALU.subtract).then_inc(s_own, w.own())
            for c in range(DC):
                for weight, n in ((w_si, 1), (w_s1, 2)):
                    dve.scalar_tensor_tensor(out=weight[1][:, c, :], in0=one_block, scalar=col[:, n, c:c + 1],
                                                 in1=weight[0][:, c, :].bitcast(F32), op0=ALU.mult, op1=ALU.subtract).then_inc(s_own, w.own())
            for n in range(4 * DC + 2 * DC):
                dve.wait_ge(s_wt, n + 1)
                src = shared[n % 2][:, 0:D]
                if n < 3 * DC:
                    m, ec = divmod(n, DC)
                    to = [wqkv[a][:, ec, m * D:(m + 1) * D] for a in range(2)]
                elif n < 4 * DC:
                    dve.tensor_copy(wo_t[:, n - 3 * DC, :], src).then_inc(s_wt_read, 1)
                    continue
                else:
                    half, ec = divmod(n - 4 * DC, DC)
                    to = [w3t[a][:, ec, half * D:(half + 1) * D] for a in range(2)]
                dve.tensor_copy(to[0], src).then_inc(s_own, w.own())
                dve.wait_ge(s_own, w.due("own"))
                dve.tensor_tensor(to[1], src, to[0].bitcast(F32), ALU.subtract).then_inc(s_wt_read, 1)
            dve.wait_ge(s_wt_read, 6 * DC)
            dve.wait_ge(s_own, w.due("own"))
            dve.memset(dmax[:, :], 0.0).then_inc(s_weights, 1)
            dve.wait_ge(s_weights, 1)

            def core(j, par, prev, now):
                head, r, _, exists = lagged(j, 0, prev, now)
                if exists:
                    dve.wait_ge(s_scores, w.due("scores", 1))
                    if r == 0:
                        dve.wait_ge(s_turned, w.due("scores_turned", NT, 2 * NT))
                    w.stand_apart()
                    dve.tensor_tensor_reduce(scores[:, head % 2, r, :], score_bank[j % 2][:, :], adj[par][:, r, :],
                                             MASK_SCALE, LOWEST, ALU.mult, ALU.max,
                                             peak[:, j % (2 * NT):j % (2 * NT) + 1]).then_inc(s_peaks, 1)
                head, c, _, exists = lagged(j, CTX_LAG, prev, now)
                if exists and head % HG == HG - 1 and c == NT - 1:
                    group = head // HG
                    dve.wait_ge(s_probs_used, w.due("summed", NT))
                    dve.reciprocal(ctx_n[:, group, :], sum_bank[:, :]).then_inc(s_own, w.own())
                    dve.wait_ge(s_own, w.due("own"))
                    dve.tensor_tensor(ctx_n[:, group, :], ctx_bank[:, :], ctx_n[:, group, :], ALU.mult)\
                        .then_inc(s_ctx_n, 1)

            def step(t, par, prev, now, nxt):
                new, old = x[1 - par], x[1 - par]
                for name, i in parts(prev, nxt):
                    if name == "core":
                        core(i, par, prev, now)
                    elif name.startswith("stats"):
                        src = x_raw if name == "stats0" else new
                        if name == "stats0":
                            dve.wait_ge(s_x_in, w.due("x_in", 16))
                        for b in range(2):
                            dve.wait_ge(s_bank_read[b], w.uses_of(b))
                        dve.wait_ge(s_own, w.due("own"))
                        for r in range(NT):
                            dve.bn_stats(stats[:, r, :], src[:, r, :]).then_inc(s_own, w.own())
                        dve.wait_ge(s_own, w.due("own"))
                        w.stand_apart()
                        for r in range(NT):
                            ins = dve.bn_aggr(mean_var[:, r, :], stats[:, r, :])
                        ins.then_inc(s_var, 1)
                    elif name.startswith("norm"):
                        src = x_raw if name == "norm0" else new
                        dve.wait_ge(s_rstd, w.due("rstd", 1))
                        for r in range(NT):
                            ins = dve.tensor_scalar(h[:, r, :], src[:, r, :], mean_var[:, r, 0:1], rstd[:, r:r + 1],
                                                    ALU.subtract, ALU.mult)
                        ins.then_inc(s_h, 1)
                    elif name.startswith("turn_h"):
                        for c in range(DC):
                            b = w.take_bank()
                            dve.wait_ge(s_bank_full[b], w.uses_of(b))
                            dve.wait_ge(s_ht1, w.due("ht1", 1))
                            dve.scalar_tensor_tensor(out=ht2[:, c, :], in0=shared[b][:, :], scalar=0.0,
                                                     in1=ht1[:, c, :].bitcast(F32), op0=ALU.max, op1=ALU.subtract)\
                                .then_inc(s_bank_read[b], 1)
                    elif name == "g":
                        if i == 0 and (prev or now):
                            for c in range(DC):
                                dve.wait_ge(s_stacks[c], w.due(f"stacks{c}", 16 * STACK_DMAS))
                        w.take_bank()
                        b = w.take_bank()
                        dve.wait_ge(s_bank_full[b], w.uses_of(b))
                        s_col = shared[b][:, D:D + 1]
                        dve.tensor_scalar(sj[:, i:i + 1], s_col, e_const[:, 0:1], None, ALU.add).then_inc(s_own, w.own())
                        dve.tensor_scalar(sj_low[:, i:i + 1], s_col, e_const[:, 0:1], 0.2, ALU.add, ALU.mult).then_inc(s_own, w.own())
                        dve.tensor_tensor(g0[:, i, :], shared[b][:, 0:D], bias0[:, :], ALU.add)\
                            .then_inc(s_bank_read[b], 1)
                    elif name == "si":
                        w.take_bank()
                        for b in range(2):
                            dve.wait_ge(s_bank_read[b], w.uses_of(b))
                        dve.wait_ge(s_own, w.due("own"))
                    elif name == "e_max":
                        dve.wait_ge(s_e_low, w.due("e_low", 1))
                        dve.scalar_tensor_tensor(out=alpha[:, i, :], in0=si[:, :], scalar=sj[:, i:i + 1],
                                                 in1=alpha[:, i, :], op0=ALU.add, op1=ALU.max).then_inc(s_e_max, 1)
                    elif name == "alpha0":
                        if i == 0:
                            for b in range(2):
                                dve.wait_ge(s_bank_read[b], w.uses_of(b))
                        dve.wait_ge(s_e_exp, w.due("e_exp", 1))
                        dve.tensor_tensor(alpha[:, i, :], alpha[:, i, :], adj_t[1 - par][:, i, :], ALU.mult)\
                            .then_inc(s_alpha0, 1)
                    elif name == "hop1":
                        b = w.take_bank()
                        dve.wait_ge(s_bank_full[b], w.uses_of(b))
                        dve.tensor_scalar(rs[:, i:i + 1], shared[b][:, D:D + 1], L0_EPS, None, ALU.add).then_inc(s_own, w.own())
                        dve.wait_ge(s_own, w.due("own"))
                        dve.reciprocal(rinv[:, i:i + 1], rs[:, i:i + 1]).then_inc(s_own, w.own())
                        dve.wait_ge(s_own, w.due("own"))
                        dve.scalar_tensor_tensor(out=u[:, i, 0:D], in0=shared[b][:, 0:D], scalar=rinv[:, i:i + 1],
                                                 in1=gg[:, i, 0:D], op0=ALU.mult, op1=ALU.add)\
                            .then_inc(s_bank_read[b], 1)
                    elif name == "hop2":
                        if i == 0 and prev:
                            dve.wait_ge(s_stored, w.due("stored", 16))
                        b = w.take_bank()
                        dve.wait_ge(s_bank_full[b], w.uses_of(b))
                        dve.scalar_tensor_tensor(out=g0[:, i, :], in0=shared[b][:, 0:D], scalar=rinv[:, i:i + 1],
                                                 in1=g0[:, i, :], op0=ALU.mult, op1=ALU.add).then_inc(s_bank_read[b], 1)
                        for b in range(2):
                            dve.wait_ge(s_bank_read[b], w.uses_of(b))
                        last = dve.scalar_tensor_tensor(out=new[:, i, :], in0=g0[:, i, :], scalar=0.0,
                                                        in1=x_raw[:, i, :], op0=ALU.max, op1=ALU.add)
                        if i == NT - 1:
                            last.then_inc(s_x1, 1)
                            dve.wait_ge(s_x1, w.due("x1", 1))
                    elif name == "deg":
                        dve.wait_ge(s_adj_in, w.due("adj_in", 16))
                        dve.tensor_reduce(deg[:, 1 - par, :], adj[1 - par][:, :, :], AX_X, ALU.add).then_inc(s_own, w.own())
                    elif name == "s1":
                        w.take_bank()
                    elif name == "t_max":
                        if i < NT - 1:
                            dve.wait_ge(s_t_tanh, w.due("t_tanh", 1))
                        else:
                            for b in range(2):
                                dve.wait_ge(s_bank_read[b], w.uses_of(b))
                        dve.scalar_tensor_tensor(out=alpha[:, i, :], in0=alpha[:, i, :], scalar=0.1,
                                                 in1=alpha[:, i, :], op0=ALU.mult, op1=ALU.max).then_inc(s_t_max, 1)
                    elif name == "alpha1":
                        dve.wait_ge(s_t_exp, w.due("t_exp", 1))
                        dve.tensor_tensor(alpha[:, i, :], alpha[:, i, :], adj_t[1 - par][:, i, :], ALU.mult)\
                            .then_inc(s_alpha1, 1)
                    elif name == "agg1":
                        b = w.take_bank()
                        dve.wait_ge(s_bank_full[b], w.uses_of(b))
                        dve.reciprocal(rinv[:, i:i + 1], shared[b][:, D:D + 1]).then_inc(s_own, w.own())
                        dve.wait_ge(s_own, w.due("own"))
                        dve.tensor_tensor(rs[:, i:i + 1], rinv[:, i:i + 1], deg[:, 1 - par, i:i + 1], ALU.mult).then_inc(s_own, w.own())
                        dve.wait_ge(s_own, w.due("own"))
                        dve.scalar_tensor_tensor(out=new[:, i, :], in0=shared[b][:, 0:D], scalar=rs[:, i:i + 1],
                                                 in1=new[:, i, :], op0=ALU.mult, op1=ALU.add)\
                            .then_inc(s_bank_read[b], 1)
                    elif name == "qk":
                        c, m = divmod(i, 2)
                        b = w.take_bank()
                        dve.wait_ge(s_bank_full[b], w.uses_of(b))
                        dve.wait_ge(s_q1, w.due("q1", 1))
                        upper, lower = (q_part, k_part)[m]
                        full, high, low = shared[b][:, :], upper[:, c, :], lower[:, c]
                        if m == 1:
                            full, high = (a.rearrange("p (t n) -> p t n", n=D) for a in (full, high))
                        dve.scalar_tensor_tensor(out=low.bitcast(F32R), in0=full, scalar=bias_qk[:, m, c:c + 1],
                                                 in1=high, op0=ALU.add, op1=ALU.subtract).then_inc(s_bank_read[b], 1)
                    elif name == "v":
                        b = w.take_bank()
                        dve.wait_ge(s_bank_full[b], w.uses_of(b))
                        dve.tensor_tensor(v[1 - par][:, 2 * i:2 * i + 2, :],
                                          shared[b][:, :].rearrange("p (k n) -> p k n", k=2),
                                          bias_v[:, :].rearrange("p (o n) -> p o n", o=1).to_broadcast([P, 2, D]),
                                          ALU.add).then_inc(s_bank_read[b], 1)
                    elif name == "out2":
                        if i == 0:
                            dve.wait_ge(s_x_bias, w.due("x_bias", 1))
                        b = w.take_bank()
                        dve.wait_ge(s_bank_full[b], w.uses_of(b))
                        dve.tensor_tensor(old[:, 2 * i:2 * i + 2, :],
                                          shared[b][:, :].rearrange("p (k n) -> p k n", k=2),
                                          old[:, 2 * i:2 * i + 2, :], ALU.add).then_inc(s_bank_read[b], 1)
                    elif name == "z":
                        if i == 0:
                            dve.tensor_scalar(dmax[:, :], deg[:, 1 - par, :], L3_EPS, None, ALU.max).then_inc(s_own, w.own())
                            dve.wait_ge(s_own, w.due("own"))
                            dve.reciprocal(dinv[:, :], dmax[:, :]).then_inc(s_own, w.own())
                            dve.wait_ge(s_own, w.due("own"))
                        w.take_bank()
                    elif name == "adj3":
                        b = w.take_bank()
                        dve.wait_ge(s_bank_full[b], w.uses_of(b))
                        dve.scalar_tensor_tensor(out=z[:, i, 0:D], in0=shared[b][:, 0:D], scalar=dinv[:, i:i + 1],
                                                 in1=z[:, i, 0:D], op0=ALU.mult, op1=ALU.add).then_inc(s_bank_read[b], 1)
                        for b in range(2):
                            dve.wait_ge(s_bank_read[b], w.uses_of(b))
                        last = dve.scalar_tensor_tensor(out=old[:, i, :], in0=z[:, i, 0:D], scalar=0.0,
                                                        in1=old[:, i, :], op0=ALU.max, op1=ALU.add)
                        if i == NT - 1:
                            last.then_inc(s_x_done, 1)
                    else:
                        w.pass_by(name)

            w.run(step)


_INS = ['x', 'adj', 'L0_gnn_Wv', 'L0_gnn_bv', 'L0_gnn_aw', 'L0_gnn_ab', 'L0_gnn_Wk', 'L0_gnn_bk', 'L1_gnn_w', 'L1_gnn_a',
        'L2_gnn_Wq', 'L2_gnn_bq', 'L2_gnn_Wk', 'L2_gnn_bk', 'L2_gnn_Wv', 'L2_gnn_bv', 'L2_gnn_Wo', 'L2_gnn_bo',
        'L3_gnn_W']
_OUTS = [((B, N, D), 'float32')]


def kernel(**inputs):
    import numpy as _np
    import concourse.bacc as _bacc
    from concourse import mybir as _mybir
    from concourse.bass_utils import run_bass_kernel_spmd as _run

    nc = _bacc.Bacc("TRN2", target_bir_lowering=False, num_devices=1, dynamic_dma_scratch_size=1024)
    arrays, args = {}, []
    for name in _INS:
        a = _np.ascontiguousarray(inputs[name])
        arrays[f"in_{name}_dram"] = a
        args.append(nc.dram_tensor(f"in_{name}_dram", a.shape, _mybir.dt.from_np(a.dtype), kind="ExternalInput").ap())
    for i, (shape, dtype) in enumerate(_OUTS):
        dt = _mybir.dt.from_np(_np.dtype(dtype))
        args.append(nc.dram_tensor(f"out_{i}_dram", shape, dt, kind="ExternalOutput").ap())
    gnn_program(nc, *args)
    r = _run(nc, [arrays], core_ids=[0])
    got = tuple(r.results[0][f"out_{i}_dram"] for i in range(len(_OUTS)))
    return got[0]
```

```python
from contextlib import ExitStack

import concourse.bass as bass
from concourse import mybir

F32 = mybir.dt.float32
F32R = mybir.dt.float32r
ALU = mybir.AluOpType
ACT = mybir.ActivationFunctionType
AX_X = mybir.AxisListType.X

P = 128
B, N, D = 16, 512, 256
NT = N // P
DC = D // P
H = 8
HD = D // H
HG = P // HD
K0 = 3
LN_EPS = 1e-5
L0_EPS = 1e-12
L3_EPS = 1e-6
LOWEST = -3.0e38
MASK_SCALE = 2.0 * HD ** -0.5
SUB = H * NT

SCORE_LAG = 4
INVERSE_LAG = SCORE_LAG + 1
TURN_LAG = SCORE_LAG + 5
PV_LAG = TURN_LAG + 1
CTX_LAG = PV_LAG + 1


ORDER = """
    stats0 stats0 stats0 stats0 2 norm0 norm0 norm0 norm0 1 turn_h0 1 g 2 si 1 g 2 g g 1 e_low e_low 1
    e_low e_low e_max e_max e_max 1 e_max e_exp 1 e_exp e_exp e_exp out2 1 out2 stats3 stats3 stats3
    stats3 1 norm3 norm3 norm3 norm3 1 turn_h3 1 z 1 z z z adj3 adj3 adj3 adj3 turn_adj turn_adj turn_adj
    turn_adj alpha0 alpha0 alpha0 alpha0 2 hop1 hop1 hop1 hop1 1 hop2 stats1 hop2 stats1 hop2 stats1 hop2
    stats1 1 norm1 norm1 norm1 norm1 deg turn_h1 1 s1 y y y y t_tanh t_tanh t_tanh t_tanh t_max 1 t_max
    t_max 1 t_max t_exp t_exp t_exp t_exp 1 alpha1 alpha1 alpha1 alpha1 1 agg1 stats2 agg1 stats2 agg1
    stats2 agg1 stats2 1 norm2 norm2 norm2 norm2 turn_h2 x_bias x_bias x_bias x_bias 1 qk qk qk qk 2 v 1
    v
"""


def build_plan():
    order, made = [], {}
    for word in ORDER.split():
        name, times = ("core", int(word)) if word.isdigit() else (word, 1)
        for _ in range(times):
            order.append((name, made.get(name, 0)))
            made[name] = made.get(name, 0) + 1
    assert made["core"] == SUB
    return order


PLAN = build_plan()
PREV = {"out2", "stats3", "norm3", "turn_h3", "z", "adj3"}
STACKED = ((0, 0), (0, 1), (1, 0))
BANKS_OF = {"turn_h0": 2, "turn_h1": 2, "turn_h2": 2, "turn_h3": 2, "g": 2, "si": 1, "z": 1, "adj3": 1,
            "turn_adj": 1, "hop1": 1, "hop2": 1, "y": 1, "s1": 1, "agg1": 1, "qk": 1, "v": 1, "out2": 1}
BANK_USES = sum(BANKS_OF.get(name, 0) for name, _ in PLAN)
SHARED = 3
assert BANK_USES % SHARED == 0 and sum(BANKS_OF.get(name, 0) for name, _ in PLAN if name in PREV) % SHARED == 0

STACK_DMAS = len(STACKED) * 2
STACK_ROWS = HD * len(STACKED)
LAYERS = 4
RAW_LOADS = 15 + 2 * K0

PER_STEP = {
    **{f"bank_{b}": BANK_USES // SHARED for b in range(SHARED)},
    "x_in": 16, "adj_in": 16, "stored": 16, "x_done": 1, "adj_masked": SUB, "scored": SUB,
    **{f"stack{head}": 16 * STACK_DMAS for head in range(H)},
    "scores": SUB, "bank_masked": SUB, "peaks": SUB, "minus_peak": SUB, "exp": SUB, "inverse": SUB, "probs": SUB, "scores_turned": SUB,
    "turned": SUB, "bank_copied": SUB, "probs_t": SUB, "probs_used": SUB // HG // 2, "weighted": SUB // HG // 2, "ctx_n": DC,
    "ctx_taken": DC, "var": LAYERS * NT, "eps": LAYERS * NT, "rstd": LAYERS * NT,
    "h": LAYERS * NT, "h2": LAYERS * NT, "ht1": LAYERS * DC,
    "sj_low": NT, "s8": NT,
    "e_low": NT, "e_max": NT, "e_exp": NT, "alpha0": NT, "t_tanh": NT, "t_max": NT, "t_exp": NT, "alpha1": NT,
    "q1": 2 * DC, "x_bias": NT, "own": None,
}


class Tally:

    def __init__(self, own_per_step=0):
        self.count, self.turn = {}, None
        self.per_step = {**PER_STEP, "own": own_per_step}

    def add(self, name, more=1):
        self.count[name] = self.count.get(name, 0) + more

    def value(self, name, lag=0):
        n = self.count.get(name, 0) - lag
        if self.turn is None:
            return max(n, 0)
        assert n > 0, name
        return self.turn * (2 * self.per_step[name]) + n

    def enter_loop(self, turn):
        self.before, self.turn = dict(self.count), turn

    def leave_loop(self, turns):
        self.turn = None
        for name, n in self.count.items():
            added = n - self.before.get(name, 0)
            assert added == 2 * self.per_step[name], (name, added, self.per_step[name])
            self.count[name] = n + (turns - 1) * added


def gnn_program(nc, x_in, adj_in, Wv0, bv0, aw0, ab0, Wk0, bk0, w1, a1, Wq, bq, Wk, bk, Wv, bv, Wo, bo, W3, out):
    with ExitStack() as ctx:
        def sb(name, shape, dt=F32):
            return ctx.enter_context(nc.sbuf_tensor(name, shape, dt))

        def bank(name):
            return ctx.enter_context(nc.psum_tensor(name, [P, N], F32))

        def sem(name):
            return ctx.enter_context(nc.semaphore(name))

        adj = [sb(f"adj{i}", [P, NT, N]) for i in range(2)]
        adj_t = [sb(f"adj_t{i}", [P, NT, N]) for i in range(2)]
        x = [sb(f"x{i}", [P, NT, D]) for i in range(2)]
        x_raw = sb("x_raw", [P, NT, D])
        v = [sb(f"v{i}", [P, NT, D]) for i in range(2)]
        deg = sb("deg", [P, 2, NT])
        alpha = sb("alpha", [P, NT, N])
        gg = sb("gg", [P, NT, 2 * D + 1])
        g0 = sb("g0", [P, NT, D])
        u = sb("u", [P, NT, D])
        h = u[:, :, :]
        ht1 = sb("ht1", [P, DC, N], F32R)
        ht2 = sb("ht2", [P, DC, N], F32R)
        z = sb("z", [P, NT, 2 * D])
        si = u[:, 0:N // D, :].rearrange("p a b -> p (a b)")
        s1 = si
        q_part = [alpha[:, 0:2, :], alpha[:, 2:4, :]]
        k_part = [z[:, 0:2, :], z[:, 2:4, :]]
        q_stack = [sb(f"q_stack{c}", [P, HG, N], F32R) for c in range(DC)]
        k_stack = [sb(f"k_stack{c}", [P, HG, N], F32R) for c in range(DC)]
        scores = sb("scores", [P, 2, NT, N])
        probs_t = sb("probs_t", [P, HG, NT, N])
        ctx_n = sb("ctx_n", [P, DC, N])
        stats = sb("stats", [P, NT, 6])
        mean_var = sb("mean_var", [P, NT, 2])
        rstd = sb("rstd", [P, NT])
        var_eps = sb("var_eps", [P, NT])
        minus_half = sb("minus_half", [P, NT])
        peak = sb("peak", [P, 2 * NT])
        minus_peak = sb("minus_peak", [P, 2 * NT])
        sums = sb("sums", [P, 2 * NT])
        inverse = sb("inverse", [P, 2 * NT])
        sj = sb("sj", [P, NT])
        sj_low = sb("sj_low", [P, NT])
        s8 = sb("s8", [P, NT])
        rs = sb("rs", [P, NT])
        rinv = sb("rinv", [P, NT])
        dinv = sb("dinv", [P, NT])
        dmax = sb("dmax", [P, NT])
        WG = 3 * D + 2
        wg = [sb(f"wg{i}", [P, DC, WG], F32R) for i in range(2)]
        wy = [sb(f"wy{i}", [P, DC, D + 2], F32R) for i in range(2)]
        w_si = [sb(f"w_si{i}", [P, DC, P], F32R) for i in range(2)]
        w_s1 = [sb(f"w_s1{i}", [P, DC, P], F32R) for i in range(2)]
        wqkv = [sb(f"wqkv{i}", [P, DC, 3 * D], F32R) for i in range(2)]
        w3t = [sb(f"w3t{i}", [P, DC, 2 * D], F32R) for i in range(2)]
        wo_t = sb("wo_t", [P, DC, D])
        bias0 = sb("bias0", [P, D])
        bias_v = sb("bias_v", [P, D])
        bias_o = sb("bias_o", [P, D])
        bias_qk = sb("bias_qk", [P, 2, DC])
        e_const = sb("e_const", [P, 1])
        col = sb("col", [P, 3, DC])
        dots = sb("dots", [P, 3])
        ident = sb("ident", [P, P])
        ones = sb("ones", [P, HD])
        raw = probs_t[:, :, :, :].rearrange("p a b c -> p (a b c)")
        at = [0]

        def room(n):
            at[0] += n
            return raw[:, at[0] - n:at[0]]

        raw_k0 = room(K0 * DC * D).rearrange("p (k c n) -> p k c n", k=K0, c=DC)
        raw_v0 = room(DC * D).rearrange("p (c n) -> p c n", c=DC)
        raw_w1 = room(DC * D).rearrange("p (c n) -> p c n", c=DC)
        raw_qkvo = room(4 * DC * D).rearrange("p (m c n) -> p m c n", m=4, c=DC)
        raw_w3 = room(DC * 2 * D).rearrange("p (c n) -> p c n", c=DC)
        raw_aw = room(2 * D)
        raw_bv0 = room(D)
        raw_a1 = room(D)
        raw_bk0 = room(K0 * D).rearrange("p (k n) -> p k n", k=K0)
        raw_ab = room(1)
        junk = z[:, 0, 0:D]
        one_block = z[:, 1, 0:P]

        score_bank = [bank("score_bank0"), bank("score_bank1")]
        turn_bank = [bank("turn_bank0"), bank("turn_bank1")]
        ctx_bank = bank("ctx_bank")
        shared = [bank(f"shared{b}") for b in range(SHARED)]

        s_x_in = sem("s_x_in")
        s_adj_in = sem("s_adj_in")
        s_stack = [sem(f"s_stack{head}") for head in range(H)]
        s_stored = sem("s_stored")
        s_scores = sem("s_scores")
        s_peaks = sem("s_peaks")
        s_minus_peak = sem("s_minus_peak")
        s_exp = sem("s_exp")
        s_inverse = sem("s_inverse")
        s_probs = sem("s_probs")
        s_turned = sem("s_turned")
        s_probs_t = sem("s_probs_t")
        s_probs_used = sem("s_probs_used")
        s_ctx_n = sem("s_ctx_n")
        s_q1 = sem("s_q1")
        s_x_bias = sem("s_x_bias")
        s_var = sem("s_var")
        s_eps = sem("s_eps")
        s_rstd = sem("s_rstd")
        s_h = sem("s_h")
        s_ht1 = sem("s_ht1")
        s_sj_low = sem("s_sj_low")
        s_s8 = sem("s_s8")
        s_e_low = sem("s_e_low")
        s_e_max = sem("s_e_max")
        s_e_exp = sem("s_e_exp")
        s_alpha0 = sem("s_alpha0")
        s_t_tanh = sem("s_t_tanh")
        s_t_max = sem("s_t_max")
        s_t_exp = sem("s_t_exp")
        s_alpha1 = sem("s_alpha1")
        s_x_done = sem("s_x_done")
        s_own = sem("s_own")
        s_bank_full = [sem(f"s_bank_full{b}") for b in range(SHARED)]
        s_bank_read = [sem(f"s_bank_read{b}") for b in range(SHARED)]
        s_raw = sem("s_raw")
        s_passed = sem("s_passed")
        s_clear = sem("s_clear")
        s_ident = sem("s_ident")
        s_half = sem("s_half")
        s_wt = sem("s_wt")
        s_wt_read = sem("s_wt_read")
        s_weights = sem("s_weights")

        class Walk:

            def __init__(self, eng, own_per_step=0):
                self.eng, self.n, self.uses = eng, Tally(own_per_step), 0

            def due(self, name, more=0, lag=0):
                self.n.add(name, more)
                return self.n.value(name, lag)

            def pass_over(self, name, more=1):
                self.n.add(name, more)

            def own(self):
                self.n.add("own")
                return 1

            def stand_apart(self):
                if self.n.turn is not None:
                    self.eng.sem_inc(s_passed, 1)

            def take_bank(self):
                b = self.uses % SHARED
                self.uses += 1
                self.n.add(f"bank_{b}")
                return b

            def uses_of(self, b, lag=0):
                return self.n.value(f"bank_{b}", lag)

            def pass_by(self, name):
                for _ in range(BANKS_OF.get(name, 0)):
                    self.take_bank()

            def run(self, step):
                step(-1, 1, False, False, True)
                step(0, 0, False, True, True)
                turns = (B - 4) // 2
                with self.eng.Fori(0, turns) as turn:
                    self.n.enter_loop(turn)
                    step(1 + 2 * turn, 1, True, True, True)
                    step(2 + 2 * turn, 0, True, True, True)
                self.n.leave_loop(turns)
                step(B - 3, 1, True, True, True)
                step(B - 2, 0, True, True, True)
                step(B - 1, 1, True, True, False)
                step(B, 0, True, False, False)

        def parts(prev, nxt):
            for name, i in PLAN:
                if name == "core" or (prev if name in PREV else nxt):
                    yield name, i

        def lagged(j, lag, prev, now):
            head, r = divmod((j - lag) % SUB, NT)
            return head, r, j < lag, (prev if j < lag else now)

        block = ctx.enter_context(nc.Block())

        @block.sync
        def _(sp):
            def rows(vector, count):
                return vector.rearrange("(o n) -> o n", o=1).to_broadcast([P, count])

            with nc.allow_non_contiguous_dma(reason="small vectors, once"):
                for dst, src in (
                    (raw_qkvo[:, 0, :, :], Wq.rearrange("(c p) n -> p c n", p=P)),
                    (raw_qkvo[:, 1, :, :], Wk.rearrange("(c p) n -> p c n", p=P)),
                    (raw_qkvo[:, 2, :, :], Wv.rearrange("(c p) n -> p c n", p=P)),
                    (raw_qkvo[:, 3, :, :], Wo.rearrange("(c p) n -> p c n", p=P)),
                    (raw_w3, W3.rearrange("(c p) n -> p c n", p=P)),
                    (raw_v0, Wv0.rearrange("(c p) n -> p c n", p=P)),
                    (raw_w1, w1.rearrange("(c p) n -> p c n", p=P)),
                    (raw_aw, aw0.rearrange("n o -> o n").to_broadcast([P, 2 * D])),
                    (raw_bv0, rows(bv0, D)),
                    (raw_a1, rows(a1, D)),
                    (raw_ab, rows(ab0, 1)),
                    (bias_v[:, :], rows(bv, D)),
                    (bias_o[:, :], rows(bo, D)),
                    (bias_qk[:, 0, :], bq.rearrange("(c p) -> p c", p=P)),
                    (bias_qk[:, 1, :], bk.rearrange("(c p) -> p c", p=P)),
                ):
                    sp.dma_start(dst, src).then_inc(s_raw, 16)
                for k in range(K0):
                    sp.dma_start(raw_k0[:, k, :, :], Wk0[k].rearrange("(c p) n -> p c n", p=P)).then_inc(s_raw, 16)
                    sp.dma_start(raw_bk0[:, k, :], bk0[k:k + 1, :].to_broadcast([P, D])).then_inc(s_raw, 16)

            x_v = x_in.rearrange("b (t p) d -> b p t d", p=P)
            adj_v = adj_in.rearrange("b (t p) n -> b p t n", p=P)
            out_v = out.rearrange("b (t p) d -> b p t d", p=P)

            def of_graph(view, g):
                if isinstance(g, int):
                    return view[g]
                return view[bass.ds(g, 1)].rearrange("o p t n -> (o p) t n")

            w = Walk(sp)

            def step(t, par, prev, now, nxt):
                if nxt:
                    sp.wait_ge(s_peaks, w.due("adj_masked", SUB, 2 * SUB))
                    w.stand_apart()
                    sp.dma_start(adj[1 - par][:, :, :], of_graph(adj_v, t + 1)).then_inc(s_adj_in, 16)
                if isinstance(t, int) and t == -1:
                    sp.dma_start(x_raw[:, :, :], of_graph(x_v, 0)).then_inc(s_x_in, 16)
                for name, i in parts(prev, nxt):
                    if name == "x_bias" and i == 0 and not (isinstance(t, int) and t + 2 >= B):
                        for b in range(SHARED):
                            sp.wait_ge(s_bank_read[b], w.uses_of(b))
                            w.stand_apart()
                        sp.dma_start(x_raw[:, :, :], of_graph(x_v, t + 2)).then_inc(s_x_in, 16)
                    if name == "qk":
                        w.take_bank()
                        if i % 2 == 0:
                            continue
                        c = i // 2
                        for b in range(SHARED):
                            sp.wait_ge(s_bank_read[b], w.uses_of(b))
                            w.stand_apart()
                        for g in range(HG):
                            sp.wait_ge(s_scores, w.due("scored", NT, SUB))
                            w.stand_apart()
                            rows_g = slice(g * HD, (g + 1) * HD)
                            for n, (q_of, k_of) in enumerate(STACKED):
                                rows_n = slice(n * HD, (n + 1) * HD)
                                sp.dma_start(q_stack[c][rows_n, g, :].bitcast(F32), q_part[q_of][rows_g, c, :])\
                                    .then_inc(s_stack[c * HG + g], 16)
                                sp.dma_start(k_stack[c][rows_n, g, :].bitcast(F32), k_part[k_of][rows_g, c, :])\
                                    .then_inc(s_stack[c * HG + g], 16)
                        continue
                    w.pass_by(name)
                    if name == "adj3" and i == NT - 1:
                        sp.wait_ge(s_x_done, w.due("x_done", 1))
                        w.stand_apart()
                        sp.dma_start(of_graph(out_v, t - 1), x[1 - par][:, :, :]).then_inc(s_stored, 16)

            w.run(step)
            sp.wait_ge(s_stored, 16 * B)

        @block.tensor
        def _(pe):
            pe.wait_ge(s_ident, 1)
            pe.wait_ge(s_raw, 16 * RAW_LOADS)
            turns = [(raw_qkvo[:, m, :, :], ec) for m in range(4) for ec in range(DC)]
            turns += [(raw_w3, ec) for ec in range(2 * DC)]
            for n, (weight, ec) in enumerate(turns):
                if n >= 2:
                    pe.wait_ge(s_wt_read, n - 1)
                for c in range(DC):
                    last = pe.transpose(shared[n % 2][:, c * P:(c + 1) * P], weight[:, c, ec * P:(ec + 1) * P],
                                        ident[:, :])
                last.then_inc(s_wt, 1)
            pe.wait_ge(s_weights, 1)

            w = Walk(pe)
            ht = (ht1, ht2)
            hop1_in, z_in = {}, {}
            turned_h = []

            def product3(to, left, right, h_is):
                first = bool(turned_h)
                if first:
                    wait_ht1()
                terms = [(0, 0), (0, 1), (1, 0)] if h_is == "left" else [(0, 0), (1, 0), (0, 1)]
                for n, (a, b) in enumerate(terms):
                    if n == 2 and first:
                        wait_ht2()
                    for c in range(DC):
                        last = pe.matmul(to, left(a, c), right(b, c), start=(n == 0 and c == 0),
                                         stop=(n == 2 and c == DC - 1))
                return last

            def wait_ht1():
                pe.wait_ge(s_ht1, w.due("ht1", DC))

            def wait_ht2():
                for b, uses in turned_h:
                    pe.wait_ge(s_bank_read[b], uses)
                turned_h.clear()

            def nodes(i):
                return lambda a, c: ht[a][:, c, i * P:(i + 1) * P]

            def all_nodes(a, c):
                return ht[a][:, c, :]

            def columns(weight, lo, hi):
                return lambda a, c: weight[a][:, c, lo:hi]

            def product_bank(cols, left, right, h_is):
                b = w.take_bank()
                pe.wait_ge(s_bank_read[b], w.uses_of(b, 1))
                product3(shared[b][:, 0:cols], left, right, h_is).then_inc(s_bank_full[b], 1)
                return b, w.uses_of(b)

            def aggregate(i, weights, values, source, purpose=None, each=None):
                b = w.take_bank()
                pe.wait_ge(s_bank_read[b], w.uses_of(b, 1))
                to = shared[b][:, 0:values.shape[-1]]
                for j in range(NT):
                    if i == 0 and purpose:
                        pe.wait_ge(source, w.due(purpose, 1))
                    elif i == 0:
                        pe.wait_ge(s_bank_read[each[j][0]], each[j][1])
                    last = pe.matmul(to, weights[:, j, i * P:(i + 1) * P], values[:, j, :],
                                     start=(j == 0), stop=(j == NT - 1))
                last.then_inc(s_bank_full[b], 1)
                return b, w.uses_of(b)

            def core(j, par, prev, now):
                head, r, _, exists = lagged(j, SCORE_LAG, prev, now)
                if exists:
                    c = head // HG
                    if r == 0:
                        pe.wait_ge(s_stack[head], w.due(f"stack{head}", 16 * STACK_DMAS))
                    pe.wait_ge(s_peaks, w.due("bank_masked", 1, 2))
                    pe.matmul(score_bank[r % 2][:, :], q_stack[c][0:STACK_ROWS, head % HG, r * P:(r + 1) * P],
                              k_stack[c][0:STACK_ROWS, head % HG, :], start=True, stop=True).then_inc(s_scores, 1)
                head, r, _, exists = lagged(j, TURN_LAG, prev, now)
                if exists:
                    pe.wait_ge(s_probs, w.due("probs", 1))
                    pe.wait_ge(s_probs_t, w.due("bank_copied", 1, 2))
                    for c in range(NT):
                        last = pe.transpose(turn_bank[r % 2][:, c * P:(c + 1) * P],
                                            scores[:, head % 2, r, c * P:(c + 1) * P], ident[:, :])
                    last.then_inc(s_turned, 1)
                head, r, older, exists = lagged(j, PV_LAG, prev, now)
                if exists and head % HG == HG - 1 and r % 2 == 1:
                    group, lo, hi = head // HG, (r - 1) * P, (r + 1) * P
                    values = v[1 - par] if older else v[par]
                    if r == 1:
                        pe.wait_ge(s_ctx_n, w.due("ctx_taken", 1, 1))
                    pe.wait_ge(s_probs_t, w.due("probs_t", (HG - 1) * NT + 2 if r == 1 else 2))
                    for c in range(NT):
                        for g in range(HG):
                            last = pe.matmul(ctx_bank[g * HD:(g + 1) * HD, lo:hi],
                                             values[:, c, group * P + g * HD:group * P + (g + 1) * HD],
                                             probs_t[:, g, c, lo:hi], start=(c == 0), stop=(c == NT - 1))
                    last.then_inc(s_probs_used, 1)

            def step(t, par, prev, now, nxt):
                for name, i in parts(prev, nxt):
                    if name == "core":
                        core(i, par, prev, now)
                    elif name.startswith("turn_h"):
                        banks = []
                        for c in range(DC):
                            b = w.take_bank()
                            turned_h.append((b, w.uses_of(b)))
                            banks.append(shared[b])
                            pe.wait_ge(s_bank_read[b], w.uses_of(b, 1))
                        for r in range(NT):
                            pe.wait_ge(s_h, w.due("h", 1))
                            for c in range(DC):
                                turn = pe.transpose(banks[c][:, r * P:(r + 1) * P], h[:, r, c * P:(c + 1) * P],
                                                    ident[:, :])
                                if r == NT - 1:
                                    turn.then_inc(s_bank_full[turned_h[c][0]], 1)
                    elif name == "g":
                        product_bank(2 * D, nodes(i), columns(wg, 0, 2 * D), "left")
                        product_bank(D + 2, nodes(i), columns(wg, 2 * D, WG), "left")
                    elif name == "si":
                        product_bank(N, columns(w_si, 0, P), all_nodes, "right")
                    elif name == "turn_adj":
                        if i == 0:
                            pe.wait_ge(s_adj_in, w.due("adj_in", 16))
                        b = w.take_bank()
                        pe.wait_ge(s_bank_read[b], w.uses_of(b, 1))
                        for r in range(NT):
                            last = pe.transpose(shared[b][:, r * P:(r + 1) * P], adj[1 - par][:, r, i * P:(i + 1) * P],
                                                ident[:, :])
                        last.then_inc(s_bank_full[b], 1)
                    elif name == "hop1":
                        hop1_in[i] = aggregate(i, alpha, gg[:, :, D:2 * D + 1], s_alpha0, "alpha0")
                    elif name == "hop2":
                        aggregate(i, alpha, u[:, :, :], s_bank_read, each=hop1_in)
                    elif name == "y":
                        product_bank(D + 2, nodes(i), columns(wy, 0, D + 2), "left")
                    elif name == "s1":
                        product_bank(N, columns(w_s1, 0, P), all_nodes, "right")
                    elif name == "agg1":
                        aggregate(i, alpha, gg[:, :, D:2 * D + 1], s_alpha1, "alpha1")
                    elif name == "qk":
                        c, m = divmod(i, 2)
                        product_bank(N, columns(wqkv, m * D + c * P, m * D + (c + 1) * P), all_nodes,
                                     "right")
                    elif name == "v":
                        b = w.take_bank()
                        pe.wait_ge(s_bank_read[b], w.uses_of(b, 1))
                        for k in range(2):
                            last = product3(shared[b][:, k * D:(k + 1) * D], nodes(2 * i + k),
                                            columns(wqkv, 2 * D, 3 * D), "left")
                        last.then_inc(s_bank_full[b], 1)
                    elif name == "out2":
                        if i == 0:
                            pe.wait_ge(s_ctx_n, w.due("ctx_n", DC))
                        b = w.take_bank()
                        pe.wait_ge(s_bank_read[b], w.uses_of(b, 1))
                        for k in range(2):
                            q = (2 * i + k) * P
                            for c in range(DC):
                                last = pe.matmul(shared[b][:, k * D:(k + 1) * D], ctx_n[:, c, q:q + P], wo_t[:, c, :],
                                                 start=(c == 0), stop=(c == DC - 1))
                        last.then_inc(s_bank_full[b], 1)
                    elif name == "z":
                        z_in[i] = product_bank(2 * D, nodes(i), columns(w3t, 0, 2 * D), "left")
                    elif name == "adj3":
                        aggregate(i, adj_t[1 - par], z[:, :, D:2 * D], s_bank_read, each=z_in)

            w.run(step)

        @block.scalar
        def _(act):
            act.wait_ge(s_raw, 16 * RAW_LOADS)
            w = Walk(act)
            si_read, s1_read = [], []

            def step(t, par, prev, now, nxt):
                for name, i in parts(prev, nxt):
                    if name == "core":
                        head, r, _, exists = lagged(i, TURN_LAG, prev, now)
                        if exists:
                            act.wait_ge(s_turned, w.due("turned", 1))
                            if head % HG == 0 and r % 2 == 0:
                                act.wait_ge(s_probs_used, w.due("probs_used", 1, 2))
                            act.copy(probs_t[:, head % HG, :, r * P:(r + 1) * P],
                                     turn_bank[r % 2][:, :].rearrange("p (c n) -> p c n", n=P)).then_inc(s_probs_t, 1)
                        head, r, _, exists = lagged(i, SCORE_LAG, prev, now)
                        if exists:
                            at = (head % 2) * NT + r
                            tile = scores[:, head % 2, r, :]
                            act.wait_ge(s_minus_peak, w.due("minus_peak", 1))
                            act.activation(tile, tile, ACT.Exp, bias=minus_peak[:, at:at + 1],
                                           accum_out=sums[:, at:at + 1]).then_inc(s_exp, 1)
                        head, r, _, exists = lagged(i, CTX_LAG, prev, now)
                        if exists and head % HG == HG - 1 and r == NT - 1:
                            act.wait_ge(s_probs_used, w.due("weighted", 2))
                            act.copy(ctx_n[:, head // HG, :], ctx_bank[:, :]).then_inc(s_ctx_n, 1)
                    elif name.startswith("turn_h"):
                        for c in range(DC):
                            b = w.take_bank()
                            act.wait_ge(s_bank_full[b], w.uses_of(b))
                            act.activation(ht1[:, c, :], shared[b][:, :], ACT.Relu).then_inc(s_ht1, 1)
                    elif name == "g":
                        b = w.take_bank()
                        act.wait_ge(s_bank_full[b], w.uses_of(b))
                        act.copy(gg[:, i, 0:2 * D], shared[b][:, :]).then_inc(s_bank_read[b], 1)
                        w.take_bank()
                    elif name == "si":
                        b = w.take_bank()
                        act.wait_ge(s_bank_full[b], w.uses_of(b))
                        act.copy(si, shared[b][:, :]).then_inc(s_bank_read[b], 1)
                        si_read[:] = [(b, w.uses_of(b))]
                    elif name == "e_low":
                        if i == 0 and now:
                            for head in range(H):
                                act.wait_ge(s_stack[head], w.due(f"stack{head}", 16 * STACK_DMAS))
                        if i == 0:
                            for b, uses in si_read:
                                act.wait_ge(s_bank_read[b], uses)
                        act.wait_ge(s_sj_low, w.due("sj_low", 1))
                        act.activation(alpha[:, i, :], si, ACT.Identity, scale=0.2,
                                       bias=sj_low[:, i:i + 1]).then_inc(s_e_low, 1)
                    elif name == "e_exp":
                        act.wait_ge(s_e_max, w.due("e_max", 1))
                        act.activation(alpha[:, i, :], alpha[:, i, :], ACT.Exp).then_inc(s_e_exp, 1)
                    elif name == "turn_adj":
                        b = w.take_bank()
                        act.wait_ge(s_bank_full[b], w.uses_of(b))
                        act.copy(adj_t[1 - par][:, i, :], shared[b][:, :]).then_inc(s_bank_read[b], 1)
                    elif name == "y":
                        b = w.take_bank()
                        act.wait_ge(s_bank_full[b], w.uses_of(b))
                        act.mul(s8[:, i:i + 1], shared[b][:, D:D + 1], 0.125).then_inc(s_s8, 1)
                        act.copy(gg[:, i, D:2 * D], shared[b][:, 0:D]).then_inc(s_bank_read[b], 1)
                    elif name == "s1":
                        b = w.take_bank()
                        act.wait_ge(s_bank_full[b], w.uses_of(b))
                        act.copy(s1, shared[b][:, :]).then_inc(s_bank_read[b], 1)
                        s1_read[:] = [(b, w.uses_of(b))]
                    elif name == "t_tanh":
                        if i == 0:
                            for b, uses in s1_read:
                                act.wait_ge(s_bank_read[b], uses)
                        act.wait_ge(s_s8, w.due("s8", 1))
                        act.activation(alpha[:, i, :], s1, ACT.Tanh, scale=0.125, bias=s8[:, i:i + 1])\
                            .then_inc(s_t_tanh, 1)
                    elif name == "t_exp":
                        act.wait_ge(s_t_max, w.due("t_max", 1))
                        act.activation(alpha[:, i, :], alpha[:, i, :], ACT.Exp, scale=8.0).then_inc(s_t_exp, 1)
                    elif name == "qk":
                        c, m = divmod(i, 2)
                        b = w.take_bank()
                        act.wait_ge(s_bank_full[b], w.uses_of(b))
                        part = (q_part, k_part)[m][0]
                        act.activation(part[:, c, :].bitcast(F32R), shared[b][:, :], ACT.Identity,
                                       bias=bias_qk[:, m, c:c + 1]).then_inc(s_q1, 1)
                    elif name == "z":
                        if i == 0 and now and not nxt:
                            for head in range(H):
                                act.wait_ge(s_stack[head], w.due(f"stack{head}", 16 * STACK_DMAS))
                        b = w.take_bank()
                        act.wait_ge(s_bank_full[b], w.uses_of(b))
                        act.copy(z[:, i, :], shared[b][:, :]).then_inc(s_bank_read[b], 1)
                    else:
                        w.pass_by(name)

            w.run(step)

        @block.gpsimd
        def _(pool):
            pool.memset(ident[:, :], 0.0).then_inc(s_clear, 1)
            pool.wait_ge(s_clear, 1)
            pool.affine_select(out=ident[:, :], in_=ident[:, :], compare_op=ALU.not_equal, fill=1.0, base=0,
                               pattern=[[-1, P]], channel_multiplier=1).then_inc(s_ident, 1)
            pool.memset(minus_half[:, :], -0.5).then_inc(s_half, 1)
            pool.wait_ge(s_half, 1)
            pool.wait_ge(s_raw, 16 * RAW_LOADS)
            w = Walk(pool)

            def step(t, par, prev, now, nxt):
                for name, i in parts(prev, nxt):
                    if name == "core":
                        head, r, _, exists = lagged(i, SCORE_LAG, prev, now)
                        if exists:
                            at = (head % 2) * NT + r
                            pool.wait_ge(s_peaks, w.due("peaks", 1))
                            w.stand_apart()
                            pool.tensor_scalar(minus_peak[:, at:at + 1], peak[:, at:at + 1], -1.0, 0.0, ALU.mult, ALU.add)\
                                .then_inc(s_minus_peak, 1)
                        head, r, _, exists = lagged(i, INVERSE_LAG, prev, now)
                        if not exists:
                            continue
                        at = (head % 2) * NT + r
                        tile = scores[:, head % 2, r, :]
                        pool.wait_ge(s_inverse, w.due("inverse", 1))
                        w.stand_apart()
                        pool.tensor_scalar(tile, tile, inverse[:, at:at + 1], 0.0, ALU.mult, ALU.add)\
                            .then_inc(s_probs, 1)
                    elif name.startswith("stats"):
                        pool.wait_ge(s_var, w.due("var", 1))
                        w.stand_apart()
                        pool.tensor_scalar(var_eps[:, i:i + 1], mean_var[:, i, 1:2], LN_EPS, 0.0, ALU.add, ALU.add)\
                            .then_inc(s_eps, 1)
                        pool.wait_ge(s_eps, w.due("eps", 1))
                        pool.tensor_tensor(rstd[:, i:i + 1], var_eps[:, i:i + 1], minus_half[:, i:i + 1], ALU.pow)\
                            .then_inc(s_rstd, 1)
                    elif name.startswith("norm"):
                        w.pass_over("h2")
                    elif name == "x_bias":
                        if i == 0:
                            pool.wait_ge(s_h, w.due("h2"))
                        pool.tensor_tensor(x[1 - par][:, i, :], x[1 - par][:, i, :], bias_o[:, :], ALU.add)\
                            .then_inc(s_x_bias, 1)

            w.run(step)

        @block.vector
        def _(dve):
            own_per_step = LAYERS * NT + NT + 2 * NT + 2 * NT + NT + 3
            w = Walk(dve, own_per_step)
            written = {}

            dve.wait_ge(s_raw, 16 * RAW_LOADS)
            dve.memset(ones[:, :], 1.0).then_inc(s_own, w.own())
            dve.memset(one_block, 1.0).then_inc(s_own, w.own())
            dve.memset(gg[:, :, 2 * D:2 * D + 1], 1.0).then_inc(s_own, w.own())
            for part in range(2):
                dve.memset(wg[part][:, :, WG - 1:WG].bitcast(F32), 0.0).then_inc(s_own, w.own())
                dve.memset(wy[part][:, :, D + 1:D + 2].bitcast(F32), 0.0).then_inc(s_own, w.own())
            for c in range(DC):
                for n, (a, b) in enumerate(((raw_v0, raw_aw[:, 0:D]), (raw_v0, raw_aw[:, D:2 * D]), (raw_w1, raw_a1))):
                    dve.tensor_tensor_reduce(junk, a[:, c, :], b, 1.0, 0.0, ALU.mult, ALU.add,
                                                 col[:, n, c:c + 1]).then_inc(s_own, w.own())
                    dve.wait_ge(s_own, w.due("own"))
            for n in range(2):
                dve.tensor_tensor_reduce(junk, raw_bv0, raw_aw[:, n * D:(n + 1) * D], 1.0, 0.0, ALU.mult, ALU.add,
                                             dots[:, n:n + 1]).then_inc(s_own, w.own())
                dve.wait_ge(s_own, w.due("own"))
            dve.tensor_tensor(dots[:, 2:3], dots[:, 0:1], dots[:, 1:2], ALU.add).then_inc(s_own, w.own())
            dve.tensor_tensor(bias0[:, :], raw_bk0[:, 0, :], raw_bk0[:, 1, :], ALU.add).then_inc(s_own, w.own())
            dve.wait_ge(s_own, w.due("own"))
            dve.tensor_tensor(e_const[:, :], dots[:, 2:3], raw_ab, ALU.add).then_inc(s_own, w.own())
            dve.tensor_tensor(bias0[:, :], bias0[:, :], raw_bk0[:, 2, :], ALU.add).then_inc(s_own, w.own())
            split = []
            for c in range(DC):
                for k, at_col in ((1, 0), (2, D), (0, 2 * D)):
                    split.append((wg, (c, at_col, D), raw_k0[:, k, c, :]))
                split.append((wg, (c, 3 * D, 1), col[:, 0, c:c + 1]))
                split.append((wy, (c, 0, D), raw_w1[:, c, :]))
                split.append((wy, (c, D, 1), col[:, 2, c:c + 1]))
            for weight, (c, lo, n), src in split:
                dve.tensor_copy(weight[0][:, c, lo:lo + n], src).then_inc(s_own, w.own())
            for c in range(DC):
                dve.tensor_scalar(w_si[0][:, c, :], one_block, col[:, 1, c:c + 1], None, ALU.mult).then_inc(s_own, w.own())
                dve.tensor_scalar(w_s1[0][:, c, :], one_block, col[:, 2, c:c + 1], None, ALU.mult).then_inc(s_own, w.own())
            dve.wait_ge(s_own, w.due("own"))
            for weight, (c, lo, n), src in split:
                dve.tensor_tensor(weight[1][:, c, lo:lo + n], src, weight[0][:, c, lo:lo + n].bitcast(F32),
                                      ALU.subtract).then_inc(s_own, w.own())
            for c in range(DC):
                for weight, n in ((w_si, 1), (w_s1, 2)):
                    dve.scalar_tensor_tensor(out=weight[1][:, c, :], in0=one_block, scalar=col[:, n, c:c + 1],
                                                 in1=weight[0][:, c, :].bitcast(F32), op0=ALU.mult, op1=ALU.subtract).then_inc(s_own, w.own())
            for n in range(4 * DC + 2 * DC):
                dve.wait_ge(s_wt, n + 1)
                src = shared[n % 2][:, 0:D]
                if n < 3 * DC:
                    m, ec = divmod(n, DC)
                    to = [wqkv[a][:, ec, m * D:(m + 1) * D] for a in range(2)]
                elif n < 4 * DC:
                    dve.tensor_copy(wo_t[:, n - 3 * DC, :], src).then_inc(s_wt_read, 1)
                    continue
                else:
                    half, ec = divmod(n - 4 * DC, DC)
                    to = [w3t[a][:, ec, half * D:(half + 1) * D] for a in range(2)]
                dve.tensor_copy(to[0], src).then_inc(s_own, w.own())
                dve.wait_ge(s_own, w.due("own"))
                dve.tensor_tensor(to[1], src, to[0].bitcast(F32), ALU.subtract).then_inc(s_wt_read, 1)
            dve.wait_ge(s_wt_read, 6 * DC)
            dve.wait_ge(s_own, w.due("own"))
            dve.memset(dmax[:, :], 0.0).then_inc(s_weights, 1)
            dve.wait_ge(s_weights, 1)

            def core(j, par, prev, now):
                head, r, older, exists = lagged(j, SCORE_LAG, prev, now)
                if exists:
                    dve.wait_ge(s_scores, w.due("scores", 1))
                    if r % 2 == 0:
                        dve.wait_ge(s_turned, w.due("scores_turned", 2, 2 * NT))
                    w.stand_apart()
                    mask = adj[1 - par] if older else adj[par]
                    at = (head % 2) * NT + r
                    dve.tensor_tensor_reduce(scores[:, head % 2, r, :], score_bank[r % 2][:, :], mask[:, r, :],
                                             MASK_SCALE, LOWEST, ALU.mult, ALU.max,
                                             peak[:, at:at + 1]).then_inc(s_peaks, 1)
                head, r, _, exists = lagged(j, INVERSE_LAG, prev, now)
                if exists:
                    at = (head % 2) * NT + r
                    dve.wait_ge(s_exp, w.due("exp", 1))
                    dve.reciprocal(inverse[:, at:at + 1], sums[:, at:at + 1]).then_inc(s_inverse, 1)

            def step(t, par, prev, now, nxt):
                new, old = x[1 - par], x[1 - par]
                for name, i in parts(prev, nxt):
                    if name == "core":
                        core(i, par, prev, now)
                    elif name.startswith("stats"):
                        src = x_raw if name in ("stats0", "stats1") else new
                        if name == "stats0":
                            if i == 0:
                                dve.wait_ge(s_x_in, w.due("x_in", 16))
                        elif name == "stats1":
                            dve.wait_ge(s_own, w.due("own"))
                        else:
                            b, uses = written[i // 2 if name == "stats3" else i]
                            dve.wait_ge(s_bank_read[b], uses)
                        dve.bn_stats(stats[:, i, :], src[:, i, :]).then_inc(s_own, w.own())
                        dve.wait_ge(s_own, w.due("own"))
                        w.stand_apart()
                        dve.bn_aggr(mean_var[:, i, :], stats[:, i, :]).then_inc(s_var, 1)
                    elif name.startswith("norm"):
                        src = x_raw if name in ("norm0", "norm1") else new
                        dve.wait_ge(s_rstd, w.due("rstd", 1))
                        dve.tensor_scalar(h[:, i, :], src[:, i, :], mean_var[:, i, 0:1], rstd[:, i:i + 1],
                                          ALU.subtract, ALU.mult).then_inc(s_h, 1)
                    elif name.startswith("turn_h"):
                        for c in range(DC):
                            b = w.take_bank()
                            dve.wait_ge(s_bank_full[b], w.uses_of(b))
                            dve.wait_ge(s_ht1, w.due("ht1", 1))
                            dve.scalar_tensor_tensor(out=ht2[:, c, :], in0=shared[b][:, :], scalar=0.0,
                                                     in1=ht1[:, c, :].bitcast(F32), op0=ALU.max, op1=ALU.subtract)\
                                .then_inc(s_bank_read[b], 1)
                    elif name == "g":
                        w.take_bank()
                        b = w.take_bank()
                        dve.wait_ge(s_bank_full[b], w.uses_of(b))
                        s_col = shared[b][:, D:D + 1]
                        dve.tensor_scalar(sj[:, i:i + 1], s_col, e_const[:, 0:1], None, ALU.add).then_inc(s_own, w.own())
                        dve.tensor_scalar(sj_low[:, i:i + 1], s_col, e_const[:, 0:1], 0.2, ALU.add, ALU.mult).then_inc(s_sj_low, 1)
                        dve.tensor_tensor(g0[:, i, :], shared[b][:, 0:D], bias0[:, :], ALU.add)\
                            .then_inc(s_bank_read[b], 1)
                    elif name == "e_max":
                        if i == 0:
                            dve.wait_ge(s_own, w.due("own"))
                        dve.wait_ge(s_e_low, w.due("e_low", 1))
                        dve.scalar_tensor_tensor(out=alpha[:, i, :], in0=si, scalar=sj[:, i:i + 1],
                                                 in1=alpha[:, i, :], op0=ALU.add, op1=ALU.max).then_inc(s_e_max, 1)
                    elif name == "alpha0":
                        if i == 0:
                            for b in range(SHARED):
                                dve.wait_ge(s_bank_read[b], w.uses_of(b))
                        dve.wait_ge(s_e_exp, w.due("e_exp", 1))
                        dve.tensor_tensor(alpha[:, i, :], alpha[:, i, :], adj_t[1 - par][:, i, :], ALU.mult)\
                            .then_inc(s_alpha0, 1)
                    elif name == "hop1":
                        b = w.take_bank()
                        dve.wait_ge(s_bank_full[b], w.uses_of(b))
                        dve.tensor_scalar(rs[:, i:i + 1], shared[b][:, D:D + 1], L0_EPS, None, ALU.add).then_inc(s_own, w.own())
                        dve.wait_ge(s_own, w.due("own"))
                        dve.reciprocal(rinv[:, i:i + 1], rs[:, i:i + 1]).then_inc(s_own, w.own())
                        dve.wait_ge(s_own, w.due("own"))
                        dve.scalar_tensor_tensor(out=u[:, i, 0:D], in0=shared[b][:, 0:D], scalar=rinv[:, i:i + 1],
                                                 in1=gg[:, i, 0:D], op0=ALU.mult, op1=ALU.add)\
                            .then_inc(s_bank_read[b], 1)
                    elif name == "hop2":
                        b = w.take_bank()
                        dve.wait_ge(s_bank_full[b], w.uses_of(b))
                        dve.scalar_tensor_tensor(out=g0[:, i, :], in0=shared[b][:, 0:D], scalar=rinv[:, i:i + 1],
                                                 in1=g0[:, i, :], op0=ALU.mult, op1=ALU.add).then_inc(s_bank_read[b], 1)
                        for b in range(SHARED):
                            dve.wait_ge(s_bank_read[b], w.uses_of(b))
                        dve.scalar_tensor_tensor(out=x_raw[:, i, :], in0=g0[:, i, :], scalar=0.0, in1=x_raw[:, i, :],
                                                 op0=ALU.max, op1=ALU.add).then_inc(s_own, w.own())
                    elif name == "deg":
                        dve.wait_ge(s_adj_in, w.due("adj_in", 16))
                        dve.tensor_reduce(deg[:, 1 - par, :], adj[1 - par][:, :, :], AX_X, ALU.add).then_inc(s_own, w.own())
                    elif name == "t_max":
                        dve.wait_ge(s_t_tanh, w.due("t_tanh", 1))
                        dve.scalar_tensor_tensor(out=alpha[:, i, :], in0=alpha[:, i, :], scalar=0.1,
                                                 in1=alpha[:, i, :], op0=ALU.mult, op1=ALU.max).then_inc(s_t_max, 1)
                    elif name == "alpha1":
                        dve.wait_ge(s_t_exp, w.due("t_exp", 1))
                        dve.tensor_tensor(alpha[:, i, :], alpha[:, i, :], adj_t[1 - par][:, i, :], ALU.mult)\
                            .then_inc(s_alpha1, 1)
                    elif name == "agg1":
                        if i == 0 and prev:
                            dve.wait_ge(s_stored, w.due("stored", 16))
                        b = w.take_bank()
                        dve.wait_ge(s_bank_full[b], w.uses_of(b))
                        dve.reciprocal(rinv[:, i:i + 1], shared[b][:, D:D + 1]).then_inc(s_own, w.own())
                        dve.wait_ge(s_own, w.due("own"))
                        dve.tensor_tensor(rs[:, i:i + 1], rinv[:, i:i + 1], deg[:, 1 - par, i:i + 1], ALU.mult).then_inc(s_own, w.own())
                        dve.wait_ge(s_own, w.due("own"))
                        dve.scalar_tensor_tensor(out=new[:, i, :], in0=shared[b][:, 0:D], scalar=rs[:, i:i + 1],
                                                 in1=x_raw[:, i, :], op0=ALU.mult, op1=ALU.add)\
                            .then_inc(s_bank_read[b], 1)
                        written[i] = (b, w.uses_of(b))
                    elif name == "qk":
                        c, m = divmod(i, 2)
                        b = w.take_bank()
                        dve.wait_ge(s_bank_full[b], w.uses_of(b))
                        dve.wait_ge(s_q1, w.due("q1", 1))
                        upper, lower = (q_part, k_part)[m]
                        dve.scalar_tensor_tensor(out=lower[:, c, :].bitcast(F32R), in0=shared[b][:, :],
                                                 scalar=bias_qk[:, m, c:c + 1], in1=upper[:, c, :], op0=ALU.add, op1=ALU.subtract).then_inc(s_bank_read[b], 1)
                    elif name == "v":
                        b = w.take_bank()
                        dve.wait_ge(s_bank_full[b], w.uses_of(b))
                        dve.tensor_tensor(v[1 - par][:, 2 * i:2 * i + 2, :],
                                          shared[b][:, :].rearrange("p (k n) -> p k n", k=2),
                                          bias_v[:, :].rearrange("p (o n) -> p o n", o=1).to_broadcast([P, 2, D]),
                                          ALU.add).then_inc(s_bank_read[b], 1)
                    elif name == "out2":
                        if i == 0:
                            dve.wait_ge(s_x_bias, w.due("x_bias", NT))
                        b = w.take_bank()
                        dve.wait_ge(s_bank_full[b], w.uses_of(b))
                        dve.tensor_tensor(old[:, 2 * i:2 * i + 2, :],
                                          shared[b][:, :].rearrange("p (k n) -> p k n", k=2),
                                          old[:, 2 * i:2 * i + 2, :], ALU.add).then_inc(s_bank_read[b], 1)
                        written[i] = (b, w.uses_of(b))
                    elif name == "z":
                        if i == 0:
                            dve.tensor_scalar(dmax[:, :], deg[:, 1 - par, :], L3_EPS, None, ALU.max).then_inc(s_own, w.own())
                            dve.wait_ge(s_own, w.due("own"))
                            dve.reciprocal(dinv[:, :], dmax[:, :]).then_inc(s_own, w.own())
                            dve.wait_ge(s_own, w.due("own"))
                        w.take_bank()
                    elif name == "adj3":
                        b = w.take_bank()
                        dve.wait_ge(s_bank_full[b], w.uses_of(b))
                        dve.scalar_tensor_tensor(out=z[:, i, 0:D], in0=shared[b][:, 0:D], scalar=dinv[:, i:i + 1],
                                                 in1=z[:, i, 0:D], op0=ALU.mult, op1=ALU.add).then_inc(s_bank_read[b], 1)
                        for b in range(SHARED):
                            dve.wait_ge(s_bank_read[b], w.uses_of(b))
                        last = dve.scalar_tensor_tensor(out=old[:, i, :], in0=z[:, i, 0:D], scalar=0.0,
                                                        in1=old[:, i, :], op0=ALU.max, op1=ALU.add)
                        if i == NT - 1:
                            last.then_inc(s_x_done, 1)
                    else:
                        w.pass_by(name)

            w.run(step)


_INS = ['x', 'adj', 'L0_gnn_Wv', 'L0_gnn_bv', 'L0_gnn_aw', 'L0_gnn_ab', 'L0_gnn_Wk', 'L0_gnn_bk', 'L1_gnn_w', 'L1_gnn_a',
        'L2_gnn_Wq', 'L2_gnn_bq', 'L2_gnn_Wk', 'L2_gnn_bk', 'L2_gnn_Wv', 'L2_gnn_bv', 'L2_gnn_Wo', 'L2_gnn_bo',
        'L3_gnn_W']
_OUTS = [((B, N, D), 'float32')]


def kernel(**inputs):
    import numpy as _np
    import concourse.bacc as _bacc
    from concourse import mybir as _mybir
    from concourse.bass_utils import run_bass_kernel_spmd as _run

    nc = _bacc.Bacc("TRN2", target_bir_lowering=False, num_devices=1, dynamic_dma_scratch_size=1024)
    arrays, args = {}, []
    for name in _INS:
        a = _np.ascontiguousarray(inputs[name])
        arrays[f"in_{name}_dram"] = a
        args.append(nc.dram_tensor(f"in_{name}_dram", a.shape, _mybir.dt.from_np(a.dtype), kind="ExternalInput").ap())
    for i, (shape, dtype) in enumerate(_OUTS):
        dt = _mybir.dt.from_np(_np.dtype(dtype))
        args.append(nc.dram_tensor(f"out_{i}_dram", shape, dt, kind="ExternalOutput").ap())
    gnn_program(nc, *args)
    r = _run(nc, [arrays], core_ids=[0])
    got = tuple(r.results[0][f"out_{i}_dram"] for i in range(len(_OUTS)))
    return got[0]
```

```python
from contextlib import ExitStack

import concourse.bass as bass
from concourse import mybir

F32 = mybir.dt.float32
F32R = mybir.dt.float32r
ALU = mybir.AluOpType
ACT = mybir.ActivationFunctionType
AX_X = mybir.AxisListType.X

P = 128
B, N, D = 16, 512, 256
NT = N // P
DC = D // P
H = 8
HD = D // H
HG = P // HD
K0 = 3
LN_EPS = 1e-5
L0_EPS = 1e-12
L3_EPS = 1e-6
LOWEST = -3.0e38
MASK_SCALE = 2.0 * HD ** -0.5
SUB = H * NT

PIECES = {"score": (SUB, 2), "inverse": (SUB, 5), "turn": (SUB, 9), "weight": (SUB // HG // 2, 2), "ctx": (DC, 1)}


ORDER = """
    inverse turn stats0 var0 score inverse stats0 var0 stats0 var0 turn score inverse norm0 norm0 norm0
    stats0 var0 score inverse norm0 turn turn_h0 score inverse turn g turn si inverse turn score turn
    score inverse g score score turn turn inverse g weight score inverse g turn inverse score weight
    e_low turn inverse e_low e_max ctx score e_low inverse e_max e_low turn e_max e_max e_exp score e_exp
    turn score inverse out2 inverse turn score out2 stats3 e_exp e_exp var3 stats3 var3 stats3 var3
    stats3 var3 norm3 norm3 turn score norm3 norm3 turn turn_h3 turn score inverse inverse z z z z turn
    score adj3 inverse score inverse adj3 x3 x3 adj3 x3 adj3 x3 turn_adj turn_adj turn_adj turn_adj
    alpha0 alpha0 alpha0 alpha0 turn score turn inverse score hop1 inverse hop1 hop1 turn score hop1 hop2
    x1 stats1 var1 inverse hop2 x1 stats1 var1 hop2 x1 stats1 var1 hop2 x1 stats1 var1 turn turn score
    norm1 norm1 inverse norm1 norm1 deg deg deg deg turn_h1 turn turn score s1 y y y y t_tanh t_tanh
    t_tanh inverse t_tanh score weight t_max t_max inverse t_max score inverse t_exp t_max t_exp t_exp
    t_exp score turn weight alpha1 alpha1 alpha1 inverse alpha1 turn ctx score agg1 stats2 var2 agg1
    stats2 var2 agg1 stats2 var2 agg1 stats2 var2 inverse turn score norm2 norm2 norm2 inverse norm2
    x_bias inverse turn_h2 x_bias x_bias turn score x_bias qk qk qk qk turn inverse score turn score
    inverse v turn score inverse v
"""


def build_plan():
    order, made = [], {}
    for name in ORDER.split():
        order.append((name, made.get(name, 0)))
        made[name] = made.get(name, 0) + 1
    assert all(made[name] == count for name, (count, _) in PIECES.items())
    assert order.index(("weight", 1)) < order.index(("ctx", 0)) < order.index(("out2", 0))
    return order


PLAN = build_plan()
PREV = {"out2", "stats3", "var3", "norm3", "turn_h3", "z", "adj3", "x3"}
STACKED = ((0, 0), (0, 1), (1, 0))
BANKS_OF = {"turn_h0": 2, "turn_h1": 2, "turn_h2": 2, "turn_h3": 2, "g": 2, "si": 1, "z": 1, "adj3": 1,
            "turn_adj": 1, "hop1": 1, "hop2": 1, "y": 1, "s1": 1, "agg1": 1, "qk": 1, "v": 1, "out2": 1}
BANK_USES = sum(BANKS_OF.get(name, 0) for name, _ in PLAN)
SHARED = 3
assert BANK_USES % SHARED == 0 and sum(BANKS_OF.get(name, 0) for name, _ in PLAN if name in PREV) % SHARED == 0

STACK_DMAS = len(STACKED) * 2
STACK_ROWS = HD * len(STACKED)
LAYERS = 4
WEIGHTS_TURNED = 4 * DC + 2 * DC
RAW_LOADS = 6 + 2 * K0
RAW_LOADS_23 = 8 + 1

PER_STEP = {
    **{f"bank_{b}": BANK_USES // SHARED for b in range(SHARED)},
    "x_in": 16, "adj_in": 16, "stored": 16, "x_done": 1, "adj_masked": SUB, "scored": SUB,
    **{f"stack{head}": 16 * STACK_DMAS for head in range(H)},
    "scores": SUB, "bank_masked": SUB, "peaks": SUB, "minus_peak": SUB, "exp": SUB, "inverse": SUB, "probs": SUB, "scores_turned": SUB,
    "turned": SUB, "bank_copied": SUB, "probs_t": SUB, "probs_used": SUB // HG // 2, "weighted": SUB // HG // 2, "ctx_n": DC,
    "ctx_taken": DC, "var": LAYERS * NT, "eps": LAYERS * NT, "rstd": LAYERS * NT,
    "h": LAYERS * NT, "h2": LAYERS * NT, "ht1": LAYERS * DC,
    "sj_low": NT, "s8": NT,
    "e_low": NT, "e_max": NT, "e_exp": NT, "alpha0": NT, "t_tanh": NT, "t_max": NT, "t_exp": NT, "alpha1": NT,
    "q1": 2 * DC, "x_bias": NT, "own": None,
}


class Tally:

    def __init__(self, own_per_step=0):
        self.count, self.turn = {}, None
        self.per_step = {**PER_STEP, "own": own_per_step}

    def add(self, name, more=1):
        self.count[name] = self.count.get(name, 0) + more

    def value(self, name, lag=0):
        n = self.count.get(name, 0) - lag
        if self.turn is None:
            return max(n, 0)
        assert n > 0, name
        return self.turn * (2 * self.per_step[name]) + n

    def enter_loop(self, turn):
        self.before, self.turn = dict(self.count), turn

    def leave_loop(self, turns):
        self.turn = None
        for name, n in self.count.items():
            added = n - self.before.get(name, 0)
            assert added == 2 * self.per_step[name], (name, added, self.per_step[name])
            self.count[name] = n + (turns - 1) * added


def gnn_program(nc, x_in, adj_in, Wv0, bv0, aw0, ab0, Wk0, bk0, w1, a1, Wq, bq, Wk, bk, Wv, bv, Wo, bo, W3, out):
    with ExitStack() as ctx:
        def sb(name, shape, dt=F32):
            return ctx.enter_context(nc.sbuf_tensor(name, shape, dt))

        def bank(name):
            return ctx.enter_context(nc.psum_tensor(name, [P, N], F32))

        def sem(name):
            return ctx.enter_context(nc.semaphore(name))

        adj = [sb(f"adj{i}", [P, NT, N]) for i in range(2)]
        adj_t = [sb(f"adj_t{i}", [P, NT, N]) for i in range(2)]
        x = [sb(f"x{i}", [P, NT, D]) for i in range(2)]
        x_raw = sb("x_raw", [P, NT, D])
        v = [sb(f"v{i}", [P, NT, D]) for i in range(2)]
        deg = sb("deg", [P, 2, NT])
        alpha = sb("alpha", [P, NT, N])
        gg = sb("gg", [P, NT, 2 * D + 1])
        g0 = sb("g0", [P, NT, D])
        u = sb("u", [P, NT, D])
        h = u[:, :, :]
        ht1 = sb("ht1", [P, DC, N], F32R)
        ht2 = sb("ht2", [P, DC, N], F32R)
        z = sb("z", [P, NT, 2 * D])
        si = u[:, 0:N // D, :].rearrange("p a b -> p (a b)")
        s1 = si
        q_part = [alpha[:, 0:2, :], alpha[:, 2:4, :]]
        k_part = [z[:, 0:2, :], z[:, 2:4, :]]
        q_stack = [sb(f"q_stack{c}", [P, HG, N], F32R) for c in range(DC)]
        k_stack = [sb(f"k_stack{c}", [P, HG, N], F32R) for c in range(DC)]
        scores = sb("scores", [P, 2, NT, N])
        probs_t = sb("probs_t", [P, HG, NT, N])
        ctx_n = sb("ctx_n", [P, DC, N])
        stats = sb("stats", [P, NT, 6])
        mean_var = sb("mean_var", [P, NT, 2])
        rstd = sb("rstd", [P, NT])
        var_eps = sb("var_eps", [P, NT])
        minus_half = sb("minus_half", [P, NT])
        peak = sb("peak", [P, 2 * NT])
        minus_peak = sb("minus_peak", [P, 2 * NT])
        sums = sb("sums", [P, 2 * NT])
        inverse = sb("inverse", [P, 2 * NT])
        sj = sb("sj", [P, NT])
        sj_low = sb("sj_low", [P, NT])
        s8 = sb("s8", [P, NT])
        rs = sb("rs", [P, NT])
        rinv = sb("rinv", [P, NT])
        dinv = sb("dinv", [P, NT])
        dmax = sb("dmax", [P, NT])
        WG = 3 * D + 2
        wg = [sb(f"wg{i}", [P, DC, WG], F32R) for i in range(2)]
        wy = [sb(f"wy{i}", [P, DC, D + 2], F32R) for i in range(2)]
        w_si = [sb(f"w_si{i}", [P, DC, P], F32R) for i in range(2)]
        w_s1 = [sb(f"w_s1{i}", [P, DC, P], F32R) for i in range(2)]
        wqkv = [sb(f"wqkv{i}", [P, DC, 3 * D], F32R) for i in range(2)]
        w3t = [sb(f"w3t{i}", [P, DC, 2 * D], F32R) for i in range(2)]
        wo_t = sb("wo_t", [P, DC, D])
        bias0 = sb("bias0", [P, D])
        bias_v = sb("bias_v", [P, D])
        bias_o = sb("bias_o", [P, D])
        bias_qk = sb("bias_qk", [P, 2, DC])
        e_const = sb("e_const", [P, 1])
        col = sb("col", [P, 3, DC])
        dots = sb("dots", [P, 3])
        ident = sb("ident", [P, P])
        ones = sb("ones", [P, HD])
        raw = probs_t[:, :, :, :].rearrange("p a b c -> p (a b c)")
        at = [0]

        def room(n):
            at[0] += n
            return raw[:, at[0] - n:at[0]]

        raw_k0 = room(K0 * DC * D).rearrange("p (k c n) -> p k c n", k=K0, c=DC)
        raw_v0 = room(DC * D).rearrange("p (c n) -> p c n", c=DC)
        raw_w1 = room(DC * D).rearrange("p (c n) -> p c n", c=DC)
        raw_qkvo = room(4 * DC * D).rearrange("p (m c n) -> p m c n", m=4, c=DC)
        raw_w3 = room(DC * 2 * D).rearrange("p (c n) -> p c n", c=DC)
        raw_aw = room(2 * D)
        raw_bv0 = room(D)
        raw_a1 = room(D)
        raw_bk0 = room(K0 * D).rearrange("p (k n) -> p k n", k=K0)
        raw_ab = room(1)
        junk = z[:, 0, 0:D]
        one_block = z[:, 1, 0:P]

        score_bank = [bank("score_bank0"), bank("score_bank1")]
        turn_bank = [bank("turn_bank0"), bank("turn_bank1")]
        ctx_bank = bank("ctx_bank")
        shared = [bank(f"shared{b}") for b in range(SHARED)]

        s_x_in = sem("s_x_in")
        s_adj_in = sem("s_adj_in")
        s_stack = [sem(f"s_stack{head}") for head in range(H)]
        s_stored = sem("s_stored")
        s_scores = sem("s_scores")
        s_peaks = sem("s_peaks")
        s_minus_peak = sem("s_minus_peak")
        s_exp = sem("s_exp")
        s_inverse = sem("s_inverse")
        s_probs = sem("s_probs")
        s_turned = sem("s_turned")
        s_probs_t = sem("s_probs_t")
        s_probs_used = sem("s_probs_used")
        s_ctx_n = sem("s_ctx_n")
        s_q1 = sem("s_q1")
        s_x_bias = sem("s_x_bias")
        s_var = sem("s_var")
        s_eps = sem("s_eps")
        s_rstd = sem("s_rstd")
        s_h = sem("s_h")
        s_ht1 = sem("s_ht1")
        s_sj_low = sem("s_sj_low")
        s_s8 = sem("s_s8")
        s_e_low = sem("s_e_low")
        s_e_max = sem("s_e_max")
        s_e_exp = sem("s_e_exp")
        s_alpha0 = sem("s_alpha0")
        s_t_tanh = sem("s_t_tanh")
        s_t_max = sem("s_t_max")
        s_t_exp = sem("s_t_exp")
        s_alpha1 = sem("s_alpha1")
        s_x_done = sem("s_x_done")
        s_own = sem("s_own")
        s_bank_full = [sem(f"s_bank_full{b}") for b in range(SHARED)]
        s_bank_read = [sem(f"s_bank_read{b}") for b in range(SHARED)]
        s_raw = sem("s_raw")
        s_raw_23 = sem("s_raw_23")
        s_passed = sem("s_passed")
        s_clear = sem("s_clear")
        s_ident = sem("s_ident")
        s_half = sem("s_half")
        s_wt = sem("s_wt")
        s_wt_read = sem("s_wt_read")
        s_weights = sem("s_weights")

        class Walk:

            def __init__(self, eng, own_per_step=0):
                self.eng, self.n, self.uses = eng, Tally(own_per_step), 0

            def due(self, name, more=0, lag=0):
                self.n.add(name, more)
                return self.n.value(name, lag)

            def pass_over(self, name, more=1):
                self.n.add(name, more)

            def own(self):
                self.n.add("own")
                return 1

            def stand_apart(self):
                if self.n.turn is not None:
                    self.eng.sem_inc(s_passed, 1)

            def take_bank(self):
                b = self.uses % SHARED
                self.uses += 1
                self.n.add(f"bank_{b}")
                return b

            def uses_of(self, b, lag=0):
                return self.n.value(f"bank_{b}", lag)

            def pass_by(self, name):
                for _ in range(BANKS_OF.get(name, 0)):
                    self.take_bank()

            def run(self, step):
                step(-1, 1, False, False, True)
                step(0, 0, False, True, True)
                turns = (B - 4) // 2
                with self.eng.Fori(0, turns) as turn:
                    self.n.enter_loop(turn)
                    step(1 + 2 * turn, 1, True, True, True)
                    step(2 + 2 * turn, 0, True, True, True)
                self.n.leave_loop(turns)
                step(B - 3, 1, True, True, True)
                step(B - 2, 0, True, True, True)
                step(B - 1, 1, True, True, False)
                step(B, 0, True, False, False)

        def parts(prev, nxt):
            for name, i in PLAN:
                if name in PIECES or (prev if name in PREV else nxt):
                    yield name, i

        def turned_with(name, i):
            return range(WEIGHTS_TURNED * i // NT, WEIGHTS_TURNED * (i + 1) // NT) if name == "g" else ()

        def piece(name, k, prev, now):
            count, older = PIECES[name]
            return (k - older) % count, k < older, (prev if k < older else now)

        block = ctx.enter_context(nc.Block())

        @block.sync
        def _(sp):
            def rows(vector, count):
                return vector.rearrange("(o n) -> o n", o=1).to_broadcast([P, count])

            x_v = x_in.rearrange("b (t p) d -> b p t d", p=P)
            adj_v = adj_in.rearrange("b (t p) n -> b p t n", p=P)
            out_v = out.rearrange("b (t p) d -> b p t d", p=P)

            def of_graph(view, g):
                if isinstance(g, int):
                    return view[g]
                return view[bass.ds(g, 1)].rearrange("o p t n -> (o p) t n")

            with nc.allow_non_contiguous_dma(reason="small vectors, once"):
                sp.dma_start(x_raw[:, :, :], of_graph(x_v, 0)).then_inc(s_x_in, 16)
                for dst, src in (
                    (raw_v0, Wv0.rearrange("(c p) n -> p c n", p=P)),
                    (raw_aw, aw0.rearrange("n o -> o n").to_broadcast([P, 2 * D])),
                    (raw_w1, w1.rearrange("(c p) n -> p c n", p=P)),
                    (raw_a1, rows(a1, D)),
                    (raw_bv0, rows(bv0, D)),
                    (raw_ab, rows(ab0, 1)),
                ):
                    sp.dma_start(dst, src).then_inc(s_raw, 16)
                for k in range(K0):
                    sp.dma_start(raw_k0[:, k, :, :], Wk0[k].rearrange("(c p) n -> p c n", p=P)).then_inc(s_raw, 16)
                    sp.dma_start(raw_bk0[:, k, :], bk0[k:k + 1, :].to_broadcast([P, D])).then_inc(s_raw, 16)
                for dst, src in (
                    (raw_qkvo[:, 0, :, :], Wq.rearrange("(c p) n -> p c n", p=P)),
                    (raw_qkvo[:, 1, :, :], Wk.rearrange("(c p) n -> p c n", p=P)),
                    (raw_qkvo[:, 2, :, :], Wv.rearrange("(c p) n -> p c n", p=P)),
                    (raw_qkvo[:, 3, :, :], Wo.rearrange("(c p) n -> p c n", p=P)),
                    (raw_w3, W3.rearrange("(c p) n -> p c n", p=P)),
                    (bias_v[:, :], rows(bv, D)),
                    (bias_o[:, :], rows(bo, D)),
                    (bias_qk[:, 0, :], bq.rearrange("(c p) -> p c", p=P)),
                    (bias_qk[:, 1, :], bk.rearrange("(c p) -> p c", p=P)),
                ):
                    sp.dma_start(dst, src).then_inc(s_raw_23, 16)

            w = Walk(sp)

            def step(t, par, prev, now, nxt):
                if nxt:
                    sp.wait_ge(s_peaks, w.due("adj_masked", SUB, 2 * SUB))
                    w.stand_apart()
                    sp.dma_start(adj[1 - par][:, :, :], of_graph(adj_v, t + 1)).then_inc(s_adj_in, 16)
                for name, i in parts(prev, nxt):
                    if name == "x_bias" and i == 0 and not (isinstance(t, int) and t + 2 >= B):
                        for b in range(SHARED):
                            sp.wait_ge(s_bank_read[b], w.uses_of(b))
                            w.stand_apart()
                        sp.dma_start(x_raw[:, :, :], of_graph(x_v, t + 2)).then_inc(s_x_in, 16)
                    if name == "qk":
                        w.take_bank()
                        if i % 2 == 0:
                            continue
                        c = i // 2
                        for b in range(SHARED):
                            sp.wait_ge(s_bank_read[b], w.uses_of(b))
                            w.stand_apart()
                        for g in range(HG):
                            sp.wait_ge(s_scores, w.due("scored", NT, SUB))
                            w.stand_apart()
                            rows_g = slice(g * HD, (g + 1) * HD)
                            for n, (q_of, k_of) in enumerate(STACKED):
                                rows_n = slice(n * HD, (n + 1) * HD)
                                sp.dma_start(q_stack[c][rows_n, g, :].bitcast(F32), q_part[q_of][rows_g, c, :])\
                                    .then_inc(s_stack[c * HG + g], 16)
                                sp.dma_start(k_stack[c][rows_n, g, :].bitcast(F32), k_part[k_of][rows_g, c, :])\
                                    .then_inc(s_stack[c * HG + g], 16)
                        continue
                    w.pass_by(name)
                    if name == "x3" and i == NT - 1:
                        sp.wait_ge(s_x_done, w.due("x_done", 1))
                        w.stand_apart()
                        sp.dma_start(of_graph(out_v, t - 1), x[1 - par][:, :, :]).then_inc(s_stored, 16)

            w.run(step)
            sp.wait_ge(s_stored, 16 * B)

        @block.tensor
        def _(pe):
            pe.wait_ge(s_ident, 1)
            turns = [(raw_qkvo[:, m, :, :], ec) for m in range(4) for ec in range(DC)]
            turns += [(raw_w3, ec) for ec in range(2 * DC)]

            def turn_weight(n):
                weight, ec = turns[n]
                if n == 0:
                    pe.wait_ge(s_raw_23, 16 * RAW_LOADS_23)
                if n >= 2:
                    pe.wait_ge(s_wt_read, n - 1)
                for c in range(DC):
                    last = pe.transpose(turn_bank[n % 2][:, c * P:(c + 1) * P], weight[:, c, ec * P:(ec + 1) * P],
                                        ident[:, :])
                last.then_inc(s_wt, 1)

            w = Walk(pe)
            ht = (ht1, ht2)
            hop1_in, z_in = {}, {}
            turned_h = []

            def product3(to, left, right, h_is):
                first = bool(turned_h)
                if first:
                    wait_ht1()
                terms = [(0, 0), (0, 1), (1, 0)] if h_is == "left" else [(0, 0), (1, 0), (0, 1)]
                for n, (a, b) in enumerate(terms):
                    if n == 2 and first:
                        wait_ht2()
                    for c in range(DC):
                        last = pe.matmul(to, left(a, c), right(b, c), start=(n == 0 and c == 0),
                                         stop=(n == 2 and c == DC - 1))
                return last

            def wait_ht1():
                pe.wait_ge(s_ht1, w.due("ht1", DC))

            def wait_ht2():
                for b, uses in turned_h:
                    pe.wait_ge(s_bank_read[b], uses)
                turned_h.clear()

            def nodes(i):
                return lambda a, c: ht[a][:, c, i * P:(i + 1) * P]

            def all_nodes(a, c):
                return ht[a][:, c, :]

            def columns(weight, lo, hi):
                return lambda a, c: weight[a][:, c, lo:hi]

            def product_bank(cols, left, right, h_is):
                b = w.take_bank()
                pe.wait_ge(s_bank_read[b], w.uses_of(b, 1))
                product3(shared[b][:, 0:cols], left, right, h_is).then_inc(s_bank_full[b], 1)
                return b, w.uses_of(b)

            def aggregate(i, weights, values, source, purpose=None, each=None):
                b = w.take_bank()
                pe.wait_ge(s_bank_read[b], w.uses_of(b, 1))
                to = shared[b][:, 0:values.shape[-1]]
                for j in range(NT):
                    if i == 0 and purpose:
                        pe.wait_ge(source, w.due(purpose, 1))
                    elif i == 0:
                        pe.wait_ge(s_bank_read[each[j][0]], each[j][1])
                    last = pe.matmul(to, weights[:, j, i * P:(i + 1) * P], values[:, j, :],
                                     start=(j == 0), stop=(j == NT - 1))
                last.then_inc(s_bank_full[b], 1)
                return b, w.uses_of(b)

            def attention(name, k, par, prev, now):
                n, older, exists = piece(name, k, prev, now)
                head, r = divmod(n, NT)
                if name == "score" and exists:
                    c = head // HG
                    if r == 0:
                        pe.wait_ge(s_stack[head], w.due(f"stack{head}", 16 * STACK_DMAS))
                    pe.wait_ge(s_peaks, w.due("bank_masked", 1, 2))
                    pe.matmul(score_bank[r % 2][:, :], q_stack[c][0:STACK_ROWS, head % HG, r * P:(r + 1) * P],
                              k_stack[c][0:STACK_ROWS, head % HG, :], start=True, stop=True).then_inc(s_scores, 1)
                if name == "turn" and exists:
                    pe.wait_ge(s_probs, w.due("probs", 1))
                    pe.wait_ge(s_probs_t, w.due("bank_copied", 1, 2))
                    for c in range(NT):
                        last = pe.transpose(turn_bank[r % 2][:, c * P:(c + 1) * P],
                                            scores[:, head % 2, r, c * P:(c + 1) * P], ident[:, :])
                    last.then_inc(s_turned, 1)
                if name == "weight" and exists:
                    group, half = divmod(n, 2)
                    lo, hi = half * 2 * P, (half + 1) * 2 * P
                    values = v[1 - par] if older else v[par]
                    if half == 0:
                        pe.wait_ge(s_ctx_n, w.due("ctx_taken", 1, 1))
                    pe.wait_ge(s_probs_t, w.due("probs_t", (HG - 1) * NT + 2 if half == 0 else 2))
                    for c in range(NT):
                        for g in range(HG):
                            last = pe.matmul(ctx_bank[g * HD:(g + 1) * HD, lo:hi],
                                             values[:, c, group * P + g * HD:group * P + (g + 1) * HD],
                                             probs_t[:, g, c, lo:hi], start=(c == 0), stop=(c == NT - 1))
                    last.then_inc(s_probs_used, 1)

            def step(t, par, prev, now, nxt):
                for name, i in parts(prev, nxt):
                    if not (prev or now):
                        for n in turned_with(name, i):
                            turn_weight(n)
                        if name == "turn_adj" and i == 0:
                            pe.wait_ge(s_wt_read, len(turns))
                    if name in PIECES:
                        attention(name, i, par, prev, now)
                    elif name.startswith("turn_h"):
                        if name == "turn_h0" and not (prev or now):
                            pe.wait_ge(s_weights, 1)
                        banks = []
                        for c in range(DC):
                            b = w.take_bank()
                            turned_h.append((b, w.uses_of(b)))
                            banks.append(shared[b])
                            pe.wait_ge(s_bank_read[b], w.uses_of(b, 1))
                        for r in range(NT):
                            pe.wait_ge(s_h, w.due("h", 1))
                            for c in range(DC):
                                turn = pe.transpose(banks[c][:, r * P:(r + 1) * P], h[:, r, c * P:(c + 1) * P],
                                                    ident[:, :])
                                if r == NT - 1:
                                    turn.then_inc(s_bank_full[turned_h[c][0]], 1)
                    elif name == "g":
                        product_bank(2 * D, nodes(i), columns(wg, 0, 2 * D), "left")
                        product_bank(D + 2, nodes(i), columns(wg, 2 * D, WG), "left")
                    elif name == "si":
                        product_bank(N, columns(w_si, 0, P), all_nodes, "right")
                    elif name == "turn_adj":
                        if i == 0:
                            pe.wait_ge(s_adj_in, w.due("adj_in", 16))
                        b = w.take_bank()
                        pe.wait_ge(s_bank_read[b], w.uses_of(b, 1))
                        for r in range(NT):
                            last = pe.transpose(shared[b][:, r * P:(r + 1) * P], adj[1 - par][:, r, i * P:(i + 1) * P],
                                                ident[:, :])
                        last.then_inc(s_bank_full[b], 1)
                    elif name == "hop1":
                        hop1_in[i] = aggregate(i, alpha, gg[:, :, D:2 * D + 1], s_alpha0, "alpha0")
                    elif name == "hop2":
                        aggregate(i, alpha, u[:, :, :], s_bank_read, each=hop1_in)
                    elif name == "y":
                        product_bank(D + 2, nodes(i), columns(wy, 0, D + 2), "left")
                    elif name == "s1":
                        product_bank(N, columns(w_s1, 0, P), all_nodes, "right")
                    elif name == "agg1":
                        aggregate(i, alpha, gg[:, :, D:2 * D + 1], s_alpha1, "alpha1")
                    elif name == "qk":
                        c, m = divmod(i, 2)
                        product_bank(N, columns(wqkv, m * D + c * P, m * D + (c + 1) * P), all_nodes,
                                     "right")
                    elif name == "v":
                        b = w.take_bank()
                        pe.wait_ge(s_bank_read[b], w.uses_of(b, 1))
                        for k in range(2):
                            last = product3(shared[b][:, k * D:(k + 1) * D], nodes(2 * i + k),
                                            columns(wqkv, 2 * D, 3 * D), "left")
                        last.then_inc(s_bank_full[b], 1)
                    elif name == "out2":
                        if i == 0:
                            pe.wait_ge(s_ctx_n, w.due("ctx_n", DC))
                        b = w.take_bank()
                        pe.wait_ge(s_bank_read[b], w.uses_of(b, 1))
                        for k in range(2):
                            q = (2 * i + k) * P
                            for c in range(DC):
                                last = pe.matmul(shared[b][:, k * D:(k + 1) * D], ctx_n[:, c, q:q + P], wo_t[:, c, :],
                                                 start=(c == 0), stop=(c == DC - 1))
                        last.then_inc(s_bank_full[b], 1)
                    elif name == "z":
                        z_in[i] = product_bank(2 * D, nodes(i), columns(w3t, 0, 2 * D), "left")
                    elif name == "adj3":
                        aggregate(i, adj_t[1 - par], z[:, :, D:2 * D], s_bank_read, each=z_in)

            w.run(step)

        @block.scalar
        def _(act):
            w = Walk(act)
            si_read, s1_read = [], []

            def step(t, par, prev, now, nxt):
                for name, i in parts(prev, nxt):
                    if name in PIECES:
                        n, _, exists = piece(name, i, prev, now)
                        head, r = divmod(n, NT)
                        if name == "turn" and exists:
                            act.wait_ge(s_turned, w.due("turned", 1))
                            if head % HG == 0 and r % 2 == 0:
                                act.wait_ge(s_probs_used, w.due("probs_used", 1, 2))
                            act.copy(probs_t[:, head % HG, :, r * P:(r + 1) * P],
                                     turn_bank[r % 2][:, :].rearrange("p (c n) -> p c n", n=P)).then_inc(s_probs_t, 1)
                        elif name == "score" and exists:
                            at = (head % 2) * NT + r
                            tile = scores[:, head % 2, r, :]
                            act.wait_ge(s_minus_peak, w.due("minus_peak", 1))
                            act.activation(tile, tile, ACT.Exp, bias=minus_peak[:, at:at + 1],
                                           accum_out=sums[:, at:at + 1]).then_inc(s_exp, 1)
                        elif name == "ctx" and exists:
                            act.wait_ge(s_probs_used, w.due("weighted", 2))
                            act.copy(ctx_n[:, n, :], ctx_bank[:, :]).then_inc(s_ctx_n, 1)
                    elif name.startswith("turn_h"):
                        for c in range(DC):
                            b = w.take_bank()
                            act.wait_ge(s_bank_full[b], w.uses_of(b))
                            act.activation(ht1[:, c, :], shared[b][:, :], ACT.Relu).then_inc(s_ht1, 1)
                    elif name == "g":
                        b = w.take_bank()
                        act.wait_ge(s_bank_full[b], w.uses_of(b))
                        act.copy(gg[:, i, 0:2 * D], shared[b][:, :]).then_inc(s_bank_read[b], 1)
                        w.take_bank()
                    elif name == "si":
                        b = w.take_bank()
                        act.wait_ge(s_bank_full[b], w.uses_of(b))
                        act.copy(si, shared[b][:, :]).then_inc(s_bank_read[b], 1)
                        si_read[:] = [(b, w.uses_of(b))]
                    elif name == "e_low":
                        if i == 0 and now:
                            for head in range(H):
                                act.wait_ge(s_stack[head], w.due(f"stack{head}", 16 * STACK_DMAS))
                        if i == 0:
                            for b, uses in si_read:
                                act.wait_ge(s_bank_read[b], uses)
                        act.wait_ge(s_sj_low, w.due("sj_low", 1))
                        act.activation(alpha[:, i, :], si, ACT.Identity, scale=0.2,
                                       bias=sj_low[:, i:i + 1]).then_inc(s_e_low, 1)
                    elif name == "e_exp":
                        act.wait_ge(s_e_max, w.due("e_max", 1))
                        act.activation(alpha[:, i, :], alpha[:, i, :], ACT.Exp).then_inc(s_e_exp, 1)
                    elif name == "turn_adj":
                        b = w.take_bank()
                        act.wait_ge(s_bank_full[b], w.uses_of(b))
                        act.copy(adj_t[1 - par][:, i, :], shared[b][:, :]).then_inc(s_bank_read[b], 1)
                    elif name == "y":
                        b = w.take_bank()
                        act.wait_ge(s_bank_full[b], w.uses_of(b))
                        act.mul(s8[:, i:i + 1], shared[b][:, D:D + 1], 0.125).then_inc(s_s8, 1)
                        act.copy(gg[:, i, D:2 * D], shared[b][:, 0:D]).then_inc(s_bank_read[b], 1)
                    elif name == "s1":
                        b = w.take_bank()
                        act.wait_ge(s_bank_full[b], w.uses_of(b))
                        act.copy(s1, shared[b][:, :]).then_inc(s_bank_read[b], 1)
                        s1_read[:] = [(b, w.uses_of(b))]
                    elif name == "t_tanh":
                        if i == 0:
                            for b, uses in s1_read:
                                act.wait_ge(s_bank_read[b], uses)
                        act.wait_ge(s_s8, w.due("s8", 1))
                        act.activation(alpha[:, i, :], s1, ACT.Tanh, scale=0.125, bias=s8[:, i:i + 1])\
                            .then_inc(s_t_tanh, 1)
                    elif name == "t_exp":
                        act.wait_ge(s_t_max, w.due("t_max", 1))
                        act.activation(alpha[:, i, :], alpha[:, i, :], ACT.Exp, scale=8.0).then_inc(s_t_exp, 1)
                    elif name == "qk":
                        if i == 0 and not (prev or now):
                            act.wait_ge(s_raw_23, 16 * RAW_LOADS_23)
                        c, m = divmod(i, 2)
                        b = w.take_bank()
                        act.wait_ge(s_bank_full[b], w.uses_of(b))
                        part = (q_part, k_part)[m][0]
                        act.activation(part[:, c, :].bitcast(F32R), shared[b][:, :], ACT.Identity,
                                       bias=bias_qk[:, m, c:c + 1]).then_inc(s_q1, 1)
                    elif name == "z":
                        if i == 0 and now and not nxt:
                            for head in range(H):
                                act.wait_ge(s_stack[head], w.due(f"stack{head}", 16 * STACK_DMAS))
                        b = w.take_bank()
                        act.wait_ge(s_bank_full[b], w.uses_of(b))
                        act.copy(z[:, i, :], shared[b][:, :]).then_inc(s_bank_read[b], 1)
                    else:
                        w.pass_by(name)

            w.run(step)

        @block.gpsimd
        def _(pool):
            pool.memset(ident[:, :], 0.0).then_inc(s_clear, 1)
            pool.wait_ge(s_clear, 1)
            pool.affine_select(out=ident[:, :], in_=ident[:, :], compare_op=ALU.not_equal, fill=1.0, base=0,
                               pattern=[[-1, P]], channel_multiplier=1).then_inc(s_ident, 1)
            pool.memset(minus_half[:, :], -0.5).then_inc(s_half, 1)
            pool.wait_ge(s_half, 1)
            w = Walk(pool)

            def step(t, par, prev, now, nxt):
                for name, i in parts(prev, nxt):
                    if name in PIECES:
                        n, _, exists = piece(name, i, prev, now)
                        head, r = divmod(n, NT)
                        at = (head % 2) * NT + r
                        tile = scores[:, head % 2, r, :]
                        if name == "score" and exists:
                            pool.wait_ge(s_peaks, w.due("peaks", 1))
                            w.stand_apart()
                            pool.tensor_scalar(minus_peak[:, at:at + 1], peak[:, at:at + 1], -1.0, 0.0, ALU.mult, ALU.add)\
                                .then_inc(s_minus_peak, 1)
                        elif name == "inverse" and exists:
                            pool.wait_ge(s_inverse, w.due("inverse", 1))
                            w.stand_apart()
                            pool.tensor_scalar(tile, tile, inverse[:, at:at + 1], 0.0, ALU.mult, ALU.add)\
                                .then_inc(s_probs, 1)
                    elif name.startswith("var"):
                        pool.wait_ge(s_var, w.due("var", 1))
                        w.stand_apart()
                        pool.tensor_scalar(var_eps[:, i:i + 1], mean_var[:, i, 1:2], LN_EPS, 0.0, ALU.add, ALU.add)\
                            .then_inc(s_eps, 1)
                        pool.wait_ge(s_eps, w.due("eps", 1))
                        pool.tensor_tensor(rstd[:, i:i + 1], var_eps[:, i:i + 1], minus_half[:, i:i + 1], ALU.pow)\
                            .then_inc(s_rstd, 1)
                    elif name.startswith("norm"):
                        w.pass_over("h2")
                    elif name == "x_bias":
                        if i == 0 and not (prev or now):
                            pool.wait_ge(s_raw_23, 16 * RAW_LOADS_23)
                        if i == 0:
                            pool.wait_ge(s_h, w.due("h2"))
                        pool.tensor_tensor(x[1 - par][:, i, :], x[1 - par][:, i, :], bias_o[:, :], ALU.add)\
                            .then_inc(s_x_bias, 1)

            w.run(step)

        @block.vector
        def _(dve):
            own_per_step = LAYERS * NT + NT + 2 * NT + 2 * NT + NT + NT + 2
            w = Walk(dve, own_per_step)
            done = {}
            written = {}

            def prepare_weights():
                dve.wait_ge(s_raw, 16 * RAW_LOADS)
                dve.memset(ones[:, :], 1.0).then_inc(s_own, w.own())
                dve.memset(one_block, 1.0).then_inc(s_own, w.own())
                dve.memset(gg[:, :, 2 * D:2 * D + 1], 1.0).then_inc(s_own, w.own())
                for part in range(2):
                    dve.memset(wg[part][:, :, WG - 1:WG].bitcast(F32), 0.0).then_inc(s_own, w.own())
                    dve.memset(wy[part][:, :, D + 1:D + 2].bitcast(F32), 0.0).then_inc(s_own, w.own())
                for c in range(DC):
                    for n, (a, b) in enumerate(((raw_v0, raw_aw[:, 0:D]), (raw_v0, raw_aw[:, D:2 * D]), (raw_w1, raw_a1))):
                        dve.tensor_tensor_reduce(junk, a[:, c, :], b, 1.0, 0.0, ALU.mult, ALU.add,
                                                     col[:, n, c:c + 1]).then_inc(s_own, w.own())
                        dve.wait_ge(s_own, w.due("own"))
                for n in range(2):
                    dve.tensor_tensor_reduce(junk, raw_bv0, raw_aw[:, n * D:(n + 1) * D], 1.0, 0.0, ALU.mult, ALU.add,
                                                 dots[:, n:n + 1]).then_inc(s_own, w.own())
                    dve.wait_ge(s_own, w.due("own"))
                dve.tensor_tensor(dots[:, 2:3], dots[:, 0:1], dots[:, 1:2], ALU.add).then_inc(s_own, w.own())
                dve.tensor_tensor(bias0[:, :], raw_bk0[:, 0, :], raw_bk0[:, 1, :], ALU.add).then_inc(s_own, w.own())
                dve.wait_ge(s_own, w.due("own"))
                dve.tensor_tensor(e_const[:, :], dots[:, 2:3], raw_ab, ALU.add).then_inc(s_own, w.own())
                dve.tensor_tensor(bias0[:, :], bias0[:, :], raw_bk0[:, 2, :], ALU.add).then_inc(s_own, w.own())
                split = []
                for c in range(DC):
                    for k, at_col in ((1, 0), (2, D), (0, 2 * D)):
                        split.append((wg, (c, at_col, D), raw_k0[:, k, c, :]))
                    split.append((wg, (c, 3 * D, 1), col[:, 0, c:c + 1]))
                    split.append((wy, (c, 0, D), raw_w1[:, c, :]))
                    split.append((wy, (c, D, 1), col[:, 2, c:c + 1]))
                for weight, (c, lo, n), src in split:
                    dve.tensor_copy(weight[0][:, c, lo:lo + n], src).then_inc(s_own, w.own())
                for c in range(DC):
                    dve.tensor_scalar(w_si[0][:, c, :], one_block, col[:, 1, c:c + 1], None, ALU.mult).then_inc(s_own, w.own())
                    dve.tensor_scalar(w_s1[0][:, c, :], one_block, col[:, 2, c:c + 1], None, ALU.mult).then_inc(s_own, w.own())
                dve.wait_ge(s_own, w.due("own"))
                for weight, (c, lo, n), src in split:
                    dve.tensor_tensor(weight[1][:, c, lo:lo + n], src, weight[0][:, c, lo:lo + n].bitcast(F32),
                                          ALU.subtract).then_inc(s_own, w.own())
                for c in range(DC):
                    for weight, n in ((w_si, 1), (w_s1, 2)):
                        dve.scalar_tensor_tensor(out=weight[1][:, c, :], in0=one_block, scalar=col[:, n, c:c + 1],
                                                     in1=weight[0][:, c, :].bitcast(F32), op0=ALU.mult, op1=ALU.subtract).then_inc(s_own, w.own())
                dve.wait_ge(s_own, w.due("own"))
                dve.memset(dmax[:, :], 0.0).then_inc(s_weights, 1)
                dve.wait_ge(s_weights, 1)

            def split_weight(n):
                if n == 0:
                    dve.wait_ge(s_raw_23, 16 * RAW_LOADS_23)
                dve.wait_ge(s_wt, n + 1)
                src = turn_bank[n % 2][:, 0:D]
                if n < 3 * DC:
                    m, ec = divmod(n, DC)
                    to = [wqkv[a][:, ec, m * D:(m + 1) * D] for a in range(2)]
                elif n < 4 * DC:
                    dve.tensor_copy(wo_t[:, n - 3 * DC, :], src).then_inc(s_wt_read, 1)
                    return
                else:
                    half, ec = divmod(n - 4 * DC, DC)
                    to = [w3t[a][:, ec, half * D:(half + 1) * D] for a in range(2)]
                dve.tensor_copy(to[0], src).then_inc(s_own, w.own())
                dve.wait_ge(s_own, w.due("own"))
                dve.tensor_tensor(to[1], src, to[0].bitcast(F32), ALU.subtract).then_inc(s_wt_read, 1)

            def attention(name, k, par, prev, now):
                n, older, exists = piece(name, k, prev, now)
                head, r = divmod(n, NT)
                at = (head % 2) * NT + r
                if name == "score" and exists:
                    dve.wait_ge(s_scores, w.due("scores", 1))
                    if r % 2 == 0:
                        dve.wait_ge(s_turned, w.due("scores_turned", 2, 2 * NT))
                    w.stand_apart()
                    mask = adj[1 - par] if older else adj[par]
                    dve.tensor_tensor_reduce(scores[:, head % 2, r, :], score_bank[r % 2][:, :], mask[:, r, :],
                                             MASK_SCALE, LOWEST, ALU.mult, ALU.max,
                                             peak[:, at:at + 1]).then_inc(s_peaks, 1)
                if name == "inverse" and exists:
                    dve.wait_ge(s_exp, w.due("exp", 1))
                    dve.reciprocal(inverse[:, at:at + 1], sums[:, at:at + 1]).then_inc(s_inverse, 1)

            def step(t, par, prev, now, nxt):
                new, old = x[1 - par], x[1 - par]
                for name, i in parts(prev, nxt):
                    if not (prev or now):
                        if name == "turn_h0":
                            prepare_weights()
                        for n in turned_with(name, i):
                            split_weight(n)
                    if name in PIECES:
                        attention(name, i, par, prev, now)
                    elif name.startswith("stats"):
                        src = x_raw if name in ("stats0", "stats1") else new
                        if name == "stats0":
                            if i == 0:
                                dve.wait_ge(s_x_in, w.due("x_in", 16))
                        elif name == "stats1":
                            dve.wait_ge(s_own, done["x1", i])
                        else:
                            b, uses = written[i // 2 if name == "stats3" else i]
                            dve.wait_ge(s_bank_read[b], uses)
                        dve.bn_stats(stats[:, i, :], src[:, i, :]).then_inc(s_own, w.own())
                        done["stats", i] = w.due("own")
                    elif name.startswith("var"):
                        dve.wait_ge(s_own, done["stats", i])
                        w.stand_apart()
                        dve.bn_aggr(mean_var[:, i, :], stats[:, i, :]).then_inc(s_var, 1)
                    elif name.startswith("norm"):
                        src = x_raw if name in ("norm0", "norm1") else new
                        dve.wait_ge(s_rstd, w.due("rstd", 1))
                        dve.tensor_scalar(h[:, i, :], src[:, i, :], mean_var[:, i, 0:1], rstd[:, i:i + 1],
                                          ALU.subtract, ALU.mult).then_inc(s_h, 1)
                    elif name.startswith("turn_h"):
                        for c in range(DC):
                            b = w.take_bank()
                            dve.wait_ge(s_bank_full[b], w.uses_of(b))
                            dve.wait_ge(s_ht1, w.due("ht1", 1))
                            dve.scalar_tensor_tensor(out=ht2[:, c, :], in0=shared[b][:, :], scalar=0.0,
                                                     in1=ht1[:, c, :].bitcast(F32), op0=ALU.max, op1=ALU.subtract)\
                                .then_inc(s_bank_read[b], 1)
                    elif name == "g":
                        w.take_bank()
                        b = w.take_bank()
                        dve.wait_ge(s_bank_full[b], w.uses_of(b))
                        s_col = shared[b][:, D:D + 1]
                        dve.tensor_scalar(sj[:, i:i + 1], s_col, e_const[:, 0:1], None, ALU.add).then_inc(s_own, w.own())
                        dve.tensor_scalar(sj_low[:, i:i + 1], s_col, e_const[:, 0:1], 0.2, ALU.add, ALU.mult).then_inc(s_sj_low, 1)
                        dve.tensor_tensor(g0[:, i, :], shared[b][:, 0:D], bias0[:, :], ALU.add)\
                            .then_inc(s_bank_read[b], 1)
                    elif name == "e_max":
                        if i == 0:
                            dve.wait_ge(s_own, w.due("own"))
                        dve.wait_ge(s_e_low, w.due("e_low", 1))
                        dve.scalar_tensor_tensor(out=alpha[:, i, :], in0=si, scalar=sj[:, i:i + 1],
                                                 in1=alpha[:, i, :], op0=ALU.add, op1=ALU.max).then_inc(s_e_max, 1)
                    elif name == "alpha0":
                        if i == 0:
                            for b in range(SHARED):
                                dve.wait_ge(s_bank_read[b], w.uses_of(b))
                        dve.wait_ge(s_e_exp, w.due("e_exp", 1))
                        dve.tensor_tensor(alpha[:, i, :], alpha[:, i, :], adj_t[1 - par][:, i, :], ALU.mult)\
                            .then_inc(s_alpha0, 1)
                    elif name == "hop1":
                        b = w.take_bank()
                        dve.wait_ge(s_bank_full[b], w.uses_of(b))
                        dve.tensor_scalar(rs[:, i:i + 1], shared[b][:, D:D + 1], L0_EPS, None, ALU.add).then_inc(s_own, w.own())
                        dve.wait_ge(s_own, w.due("own"))
                        dve.reciprocal(rinv[:, i:i + 1], rs[:, i:i + 1]).then_inc(s_own, w.own())
                        dve.wait_ge(s_own, w.due("own"))
                        dve.scalar_tensor_tensor(out=u[:, i, 0:D], in0=shared[b][:, 0:D], scalar=rinv[:, i:i + 1],
                                                 in1=gg[:, i, 0:D], op0=ALU.mult, op1=ALU.add)\
                            .then_inc(s_bank_read[b], 1)
                    elif name == "hop2":
                        b = w.take_bank()
                        dve.wait_ge(s_bank_full[b], w.uses_of(b))
                        dve.scalar_tensor_tensor(out=g0[:, i, :], in0=shared[b][:, 0:D], scalar=rinv[:, i:i + 1],
                                                 in1=g0[:, i, :], op0=ALU.mult, op1=ALU.add).then_inc(s_bank_read[b], 1)
                        done["hop2", i] = (b, w.uses_of(b))
                    elif name == "x1":
                        b, uses = done["hop2", i]
                        dve.wait_ge(s_bank_read[b], uses)
                        dve.scalar_tensor_tensor(out=x_raw[:, i, :], in0=g0[:, i, :], scalar=0.0, in1=x_raw[:, i, :],
                                                 op0=ALU.max, op1=ALU.add).then_inc(s_own, w.own())
                        done["x1", i] = w.due("own")
                    elif name == "deg":
                        if i == 0:
                            dve.wait_ge(s_adj_in, w.due("adj_in", 16))
                        dve.tensor_reduce(deg[:, 1 - par, i:i + 1], adj[1 - par][:, i, :], AX_X, ALU.add)\
                            .then_inc(s_own, w.own())
                    elif name == "t_max":
                        dve.wait_ge(s_t_tanh, w.due("t_tanh", 1))
                        dve.scalar_tensor_tensor(out=alpha[:, i, :], in0=alpha[:, i, :], scalar=0.1,
                                                 in1=alpha[:, i, :], op0=ALU.mult, op1=ALU.max).then_inc(s_t_max, 1)
                    elif name == "alpha1":
                        dve.wait_ge(s_t_exp, w.due("t_exp", 1))
                        dve.tensor_tensor(alpha[:, i, :], alpha[:, i, :], adj_t[1 - par][:, i, :], ALU.mult)\
                            .then_inc(s_alpha1, 1)
                    elif name == "agg1":
                        if i == 0 and prev:
                            dve.wait_ge(s_stored, w.due("stored", 16))
                        b = w.take_bank()
                        dve.wait_ge(s_bank_full[b], w.uses_of(b))
                        dve.reciprocal(rinv[:, i:i + 1], shared[b][:, D:D + 1]).then_inc(s_own, w.own())
                        dve.wait_ge(s_own, w.due("own"))
                        dve.tensor_tensor(rs[:, i:i + 1], rinv[:, i:i + 1], deg[:, 1 - par, i:i + 1], ALU.mult).then_inc(s_own, w.own())
                        dve.wait_ge(s_own, w.due("own"))
                        dve.scalar_tensor_tensor(out=new[:, i, :], in0=shared[b][:, 0:D], scalar=rs[:, i:i + 1],
                                                 in1=x_raw[:, i, :], op0=ALU.mult, op1=ALU.add)\
                            .then_inc(s_bank_read[b], 1)
                        written[i] = (b, w.uses_of(b))
                    elif name == "qk":
                        c, m = divmod(i, 2)
                        b = w.take_bank()
                        dve.wait_ge(s_bank_full[b], w.uses_of(b))
                        dve.wait_ge(s_q1, w.due("q1", 1))
                        upper, lower = (q_part, k_part)[m]
                        dve.scalar_tensor_tensor(out=lower[:, c, :].bitcast(F32R), in0=shared[b][:, :],
                                                 scalar=bias_qk[:, m, c:c + 1], in1=upper[:, c, :], op0=ALU.add, op1=ALU.subtract).then_inc(s_bank_read[b], 1)
                    elif name == "v":
                        b = w.take_bank()
                        dve.wait_ge(s_bank_full[b], w.uses_of(b))
                        dve.tensor_tensor(v[1 - par][:, 2 * i:2 * i + 2, :],
                                          shared[b][:, :].rearrange("p (k n) -> p k n", k=2),
                                          bias_v[:, :].rearrange("p (o n) -> p o n", o=1).to_broadcast([P, 2, D]),
                                          ALU.add).then_inc(s_bank_read[b], 1)
                    elif name == "out2":
                        if i == 0:
                            dve.wait_ge(s_x_bias, w.due("x_bias", NT))
                        b = w.take_bank()
                        dve.wait_ge(s_bank_full[b], w.uses_of(b))
                        dve.tensor_tensor(old[:, 2 * i:2 * i + 2, :],
                                          shared[b][:, :].rearrange("p (k n) -> p k n", k=2),
                                          old[:, 2 * i:2 * i + 2, :], ALU.add).then_inc(s_bank_read[b], 1)
                        written[i] = (b, w.uses_of(b))
                    elif name == "z":
                        if i == 0:
                            dve.tensor_scalar(dmax[:, :], deg[:, 1 - par, :], L3_EPS, None, ALU.max).then_inc(s_own, w.own())
                            dve.wait_ge(s_own, w.due("own"))
                            dve.reciprocal(dinv[:, :], dmax[:, :]).then_inc(s_own, w.own())
                            dve.wait_ge(s_own, w.due("own"))
                        w.take_bank()
                    elif name == "adj3":
                        b = w.take_bank()
                        dve.wait_ge(s_bank_full[b], w.uses_of(b))
                        dve.scalar_tensor_tensor(out=z[:, i, 0:D], in0=shared[b][:, 0:D], scalar=dinv[:, i:i + 1],
                                                 in1=z[:, i, 0:D], op0=ALU.mult, op1=ALU.add).then_inc(s_bank_read[b], 1)
                        done["adj3", i] = (b, w.uses_of(b))
                    elif name == "x3":
                        b, uses = done["adj3", i]
                        dve.wait_ge(s_bank_read[b], uses)
                        last = dve.scalar_tensor_tensor(out=old[:, i, :], in0=z[:, i, 0:D], scalar=0.0,
                                                        in1=old[:, i, :], op0=ALU.max, op1=ALU.add)
                        if i == NT - 1:
                            last.then_inc(s_x_done, 1)
                    else:
                        w.pass_by(name)

            w.run(step)


_INS = ['x', 'adj', 'L0_gnn_Wv', 'L0_gnn_bv', 'L0_gnn_aw', 'L0_gnn_ab', 'L0_gnn_Wk', 'L0_gnn_bk', 'L1_gnn_w', 'L1_gnn_a',
        'L2_gnn_Wq', 'L2_gnn_bq', 'L2_gnn_Wk', 'L2_gnn_bk', 'L2_gnn_Wv', 'L2_gnn_bv', 'L2_gnn_Wo', 'L2_gnn_bo',
        'L3_gnn_W']
_OUTS = [((B, N, D), 'float32')]


def kernel(**inputs):
    import numpy as _np
    import concourse.bacc as _bacc
    from concourse import mybir as _mybir
    from concourse.bass_utils import run_bass_kernel_spmd as _run

    nc = _bacc.Bacc("TRN2", target_bir_lowering=False, num_devices=1, dynamic_dma_scratch_size=1024)
    arrays, args = {}, []
    for name in _INS:
        a = _np.ascontiguousarray(inputs[name])
        arrays[f"in_{name}_dram"] = a
        args.append(nc.dram_tensor(f"in_{name}_dram", a.shape, _mybir.dt.from_np(a.dtype), kind="ExternalInput").ap())
    for i, (shape, dtype) in enumerate(_OUTS):
        dt = _mybir.dt.from_np(_np.dtype(dtype))
        args.append(nc.dram_tensor(f"out_{i}_dram", shape, dt, kind="ExternalOutput").ap())
    gnn_program(nc, *args)
    r = _run(nc, [arrays], core_ids=[0])
    got = tuple(r.results[0][f"out_{i}_dram"] for i in range(len(_OUTS)))
    return got[0]
```
